# Optimizing a Trainium2 kernel written in Bass

```python
import numpy as np
import jax
import jax.numpy as jnp

def _softmax(x, axis=-1):
    return jax.nn.softmax(x, axis=axis)

def _gelu(x):
    return jax.nn.gelu(x, approximate=True)

def _silu(x):
    return jax.nn.silu(x)

def _sigmoid(x):
    return jax.nn.sigmoid(x)

def _layernorm(x, axis=-1, eps=1e-05):
    m = jnp.mean(x, axis=axis, keepdims=True)
    v = jnp.var(x, axis=axis, keepdims=True)
    return (x - m) / jnp.sqrt(v + eps)

def _scatter_add(tgt, idx, src, axis=0):
    return tgt.at[idx].add(src)

def _segment_sum(src, seg, n):
    return jax.ops.segment_sum(src, seg, n)
kernel_name = 'mk_gnn_preln_d4_gnn_r16_3ef119'

def setup_inputs(seed: int=0):
    np.random.seed(seed)
    _w = jnp.asarray

    def _rec_inputs():
        import jax
        import jax.numpy as jnp
        _gk = jax.random.key(seed)
        x = -0.0003713 + 1 * jax.random.normal(jax.random.fold_in(_gk, 1), (6250, 128), jnp.float32)
        src = jax.random.randint(jax.random.fold_in(_gk, 2), (100000,), 0, 6250, jnp.int32)
        dst = jax.random.randint(jax.random.fold_in(_gk, 3), (100000,), 0, 6250, jnp.int32)
        _o = jnp.argsort(dst, stable=True)
        src = src[_o]
        dst = dst[_o]
        edge_attr_32 = -1.78115e-05 + 1.00007 * jax.random.normal(jax.random.fold_in(_gk, 12), (100000, 32), jnp.float32)
        edge_attr_32_n2 = -1.78115e-05 + 1.00007 * jax.random.normal(jax.random.fold_in(_gk, 13), (100000, 32), jnp.float32)
        edge_attr_64 = 0.000133148 + 1.00009 * jax.random.normal(jax.random.fold_in(_gk, 14), (100000, 64), jnp.float32)
        edge_attr_64_n2 = 0.000133148 + 1.00009 * jax.random.normal(jax.random.fold_in(_gk, 15), (100000, 64), jnp.float32)
        edge_type_16 = jax.random.randint(jax.random.fold_in(_gk, 17), (100000,), 0, 16, jnp.int32)
        edge_weight = jax.random.uniform(jax.random.fold_in(_gk, 18), (100000,), jnp.float32, 0.0, 0.999999)
        return (x, src, dst, edge_attr_32, edge_attr_32_n2, edge_attr_64, edge_attr_64_n2, edge_type_16, edge_weight)
    x, src, dst, edge_attr_32, edge_attr_32_n2, edge_attr_64, edge_attr_64_n2, edge_type_16, edge_weight = _rec_inputs()

    def _L0_gnn_setup():
        import jax, jax.numpy as jnp
        import numpy as np
        N_NODES = 6250
        N_EDGES = 625000
        D_FEAT = 128
        key = jax.random.key(seed)
        k1, k2, k3, k4 = jax.random.split(key, 4)
        feat = jax.random.normal(k1, (N_NODES, D_FEAT), dtype=jnp.float32)
        src = jax.random.randint(k2, (N_EDGES,), 0, N_NODES, dtype=jnp.int32)
        dst = jax.random.randint(k3, (N_EDGES,), 0, N_NODES, dtype=jnp.int32)
        edge_weight = jax.random.uniform(k4, (N_EDGES,), dtype=jnp.float32)
        eps = jnp.zeros((1,), dtype=jnp.float32)
        return {'feat': feat, 'src': src, 'dst': dst, 'edge_weight': edge_weight, 'eps': eps}
    _L0_gnn_all = _L0_gnn_setup()
    _L0_gnn_in = {k: v for k, v in _L0_gnn_all.items() if k in ('eps',)}
    del _L0_gnn_all

    def _L1_gnn_setup():
        import jax, jax.numpy as jnp
        import numpy as np
        N_NODES = 3125
        N_EDGES = 100000
        D_IN = 128
        D_OUT = 128
        EDGE_DIM = 64
        NUM_LAYERS = 3

        def _gru_cell(m, h, w_ih, w_hh, b_ih, b_hh):
            gi = m @ w_ih.T + b_ih
            gh = h @ w_hh.T + b_hh
            i_r, i_z, i_n = jnp.split(gi, 3, axis=1)
            h_r, h_z, h_n = jnp.split(gh, 3, axis=1)
            r = jax.nn.sigmoid(i_r + h_r)
            u = jax.nn.sigmoid(i_z + h_z)
            n = jnp.tanh(i_n + r * h_n)
            return (1.0 - u) * n + u * h
        key = jax.random.key(seed)
        ks = jax.random.split(key, 12)
        x = jax.random.normal(ks[0], (N_NODES, D_IN), dtype=jnp.float32)
        edge_index = jax.random.randint(ks[1], (2, N_EDGES), 0, N_NODES, dtype=jnp.int64)
        edge_attr = jax.random.normal(ks[2], (N_EDGES, EDGE_DIM), dtype=jnp.float32)
        z = jax.random.normal(ks[3], (N_EDGES, EDGE_DIM), dtype=jnp.float32)
        s_in = 1.0 / np.sqrt(D_IN)
        W_node = jax.random.uniform(ks[4], (D_IN, D_OUT), jnp.float32, -s_in, s_in)
        b_node = jax.random.uniform(ks[5], (D_OUT,), jnp.float32, -s_in, s_in)
        s_o = 1.0 / np.sqrt(D_OUT)
        conv_weight = jax.random.uniform(ks[6], (NUM_LAYERS, D_OUT, D_OUT), jnp.float32, -s_o, s_o)
        w_ih = jax.random.uniform(ks[7], (3 * D_OUT, D_OUT), jnp.float32, -s_o, s_o)
        w_hh = jax.random.uniform(ks[8], (3 * D_OUT, D_OUT), jnp.float32, -s_o, s_o)
        b_ih = jax.random.uniform(ks[9], (3 * D_OUT,), jnp.float32, -s_o, s_o)
        b_hh = jax.random.uniform(ks[10], (3 * D_OUT,), jnp.float32, -s_o, s_o)
        return {'x': x, 'edge_index': edge_index, 'edge_attr': edge_attr, 'z': z, 'W_node': W_node, 'b_node': b_node, 'conv_weight': conv_weight, 'w_ih': w_ih, 'w_hh': w_hh, 'b_ih': b_ih, 'b_hh': b_hh}
    _L1_gnn_all = _L1_gnn_setup()
    _L1_gnn_in = {k: v for k, v in _L1_gnn_all.items() if k in ('W_node', 'b_node', 'conv_weight', 'w_ih', 'w_hh', 'b_ih', 'b_hh')}
    del _L1_gnn_all

    def _L2_gnn_setup():
        import jax, jax.numpy as jnp
        import numpy as np
        N = 3125
        E = 25000
        D_NODE = 128
        D_EDGE = 32
        D_OUT = 128
        R = 16
        B = 8
        key = jax.random.key(seed)
        ks = jax.random.split(key, 12)
        s = 0.05
        return {'vfts': jax.random.normal(ks[0], (N, D_NODE), dtype=jnp.float32), 'adjs': jax.random.randint(ks[1], (2, E), 0, N, dtype=jnp.int32), 'rels': jax.random.randint(ks[2], (E,), 0, R, dtype=jnp.int32), 'embed_rels': jax.random.normal(ks[3], (E, D_EDGE), dtype=jnp.float32), 'embed_rels_target': jax.random.normal(ks[4], (E, D_EDGE), dtype=jnp.float32), 'weight': jax.random.normal(ks[5], (B, D_NODE, D_OUT), dtype=jnp.float32) * s, 'comp': jax.random.normal(ks[6], (R, B), dtype=jnp.float32) * s, 'attn_w1': jax.random.normal(ks[7], (2 * D_NODE + 2 * D_EDGE, D_OUT), dtype=jnp.float32) * s, 'attn_b1': jnp.zeros((D_OUT,), dtype=jnp.float32), 'attn_w2': jax.random.normal(ks[8], (D_OUT, 1), dtype=jnp.float32) * s, 'attn_b2': jnp.zeros((1,), dtype=jnp.float32), 'update': jax.random.normal(ks[9], (D_NODE, D_OUT), dtype=jnp.float32) * s}
    _L2_gnn_all = _L2_gnn_setup()
    _L2_gnn_in = {k: v for k, v in _L2_gnn_all.items() if k in ('weight', 'comp', 'attn_w1', 'attn_b1', 'attn_w2', 'attn_b2', 'update')}
    del _L2_gnn_all

    def _L3_gnn_setup():
        import jax, jax.numpy as jnp
        import numpy as np
        N_NODES = 3125
        N_EDGES = 40000
        IN_CH = 128
        OUT_CH = 128
        key = jax.random.key(seed)
        k1, k2, k3, k4 = jax.random.split(key, 4)
        x = jax.random.normal(k1, (N_NODES, IN_CH), dtype=jnp.float32)
        edge_index = jax.random.randint(k2, (2, N_EDGES), 0, N_NODES, dtype=jnp.int32)
        bound = 1.0 / np.sqrt(IN_CH)
        W = jax.random.uniform(k3, (OUT_CH, IN_CH), minval=-bound, maxval=bound, dtype=jnp.float32)
        b = jax.random.uniform(k4, (OUT_CH,), minval=-bound, maxval=bound, dtype=jnp.float32)
        return {'x': x, 'edge_index': edge_index, 'W': W, 'b': b}
    _L3_gnn_all = _L3_gnn_setup()
    _L3_gnn_in = {k: v for k, v in _L3_gnn_all.items() if k in ('W', 'b')}
    del _L3_gnn_all
    return {'x': x, 'src': src, 'dst': dst, 'edge_attr_32': edge_attr_32, 'edge_attr_32_n2': edge_attr_32_n2, 'edge_attr_64': edge_attr_64, 'edge_attr_64_n2': edge_attr_64_n2, 'edge_type_16': edge_type_16, 'edge_weight': edge_weight, 'L0_gnn_eps': _L0_gnn_in['eps'], 'L1_gnn_W_node': _L1_gnn_in['W_node'], 'L1_gnn_b_node': _L1_gnn_in['b_node'], 'L1_gnn_conv_weight': _L1_gnn_in['conv_weight'], 'L1_gnn_w_ih': _L1_gnn_in['w_ih'], 'L1_gnn_w_hh': _L1_gnn_in['w_hh'], 'L1_gnn_b_ih': _L1_gnn_in['b_ih'], 'L1_gnn_b_hh': _L1_gnn_in['b_hh'], 'L2_gnn_weight': _L2_gnn_in['weight'], 'L2_gnn_comp': _L2_gnn_in['comp'], 'L2_gnn_attn_w1': _L2_gnn_in['attn_w1'], 'L2_gnn_attn_b1': _L2_gnn_in['attn_b1'], 'L2_gnn_attn_w2': _L2_gnn_in['attn_w2'], 'L2_gnn_attn_b2': _L2_gnn_in['attn_b2'], 'L2_gnn_update': _L2_gnn_in['update'], 'L3_gnn_W': _L3_gnn_in['W'], 'L3_gnn_b': _L3_gnn_in['b']}

def reference(x, src, dst, edge_attr_32, edge_attr_32_n2, edge_attr_64, edge_attr_64_n2, edge_type_16, edge_weight, L0_gnn_eps, L1_gnn_W_node, L1_gnn_b_node, L1_gnn_conv_weight, L1_gnn_w_ih, L1_gnn_w_hh, L1_gnn_b_ih, L1_gnn_b_hh, L2_gnn_weight, L2_gnn_comp, L2_gnn_attn_w1, L2_gnn_attn_b1, L2_gnn_attn_w2, L2_gnn_attn_b2, L2_gnn_update, L3_gnn_W, L3_gnn_b):
    import jax
    import jax.numpy as jnp

    def _L0_gnn_ref(feat, src, dst, edge_weight, eps):
        import jax, jax.numpy as jnp
        import numpy as np
        N_NODES = 6250
        N_EDGES = 625000
        D_FEAT = 128
        messages = feat[src] * edge_weight[:, None]
        neigh = jax.ops.segment_sum(messages, dst, num_segments=feat.shape[0])
        return (1.0 + eps) * feat + neigh

    def _L1_gnn_ref(x, edge_index, edge_attr, z, W_node, b_node, conv_weight, w_ih, w_hh, b_ih, b_hh):
        import jax, jax.numpy as jnp
        import numpy as np
        N_NODES = 3125
        N_EDGES = 100000
        D_IN = 128
        D_OUT = 128
        EDGE_DIM = 64
        NUM_LAYERS = 3

        def _gru_cell(m, h, w_ih, w_hh, b_ih, b_hh):
            gi = m @ w_ih.T + b_ih
            gh = h @ w_hh.T + b_hh
            i_r, i_z, i_n = jnp.split(gi, 3, axis=1)
            h_r, h_z, h_n = jnp.split(gh, 3, axis=1)
            r = jax.nn.sigmoid(i_r + h_r)
            u = jax.nn.sigmoid(i_z + h_z)
            n = jnp.tanh(i_n + r * h_n)
            return (1.0 - u) * n + u * h
        h = jax.nn.relu(x @ W_node + b_node)
        edge_weight = jnp.sum(z * edge_attr, axis=1)
        src, dst = (edge_index[0], edge_index[1])
        n_nodes = h.shape[0]
        for i in range(NUM_LAYERS):
            m = h @ conv_weight[i]
            msg = edge_weight[:, None] * m[src]
            agg = jax.ops.segment_sum(msg, dst, num_segments=n_nodes)
            h = _gru_cell(agg, h, w_ih, w_hh, b_ih, b_hh)
        return h

    def _L2_gnn_ref(vfts, adjs, rels, embed_rels, embed_rels_target, weight, comp, attn_w1, attn_b1, attn_w2, attn_b2, update):
        import jax, jax.numpy as jnp
        import numpy as np
        N = 3125
        E = 25000
        D_NODE = 128
        D_EDGE = 32
        D_OUT = 128
        R = 16
        B = 8
        src, dst = (adjs[0], adjs[1])
        erps = jnp.concatenate((vfts[src], vfts[dst], embed_rels, embed_rels_target), axis=1)
        h = jax.nn.relu(erps @ attn_w1 + attn_b1)
        alphas = jax.nn.sigmoid(h @ attn_w2 + attn_b2)
        w_rel = (comp @ weight.reshape(B, D_NODE * D_OUT)).reshape(R, D_NODE, D_OUT)
        srcs_dense = jnp.einsum('nd,rdo->rno', vfts, w_rel)
        srcs = alphas[rels] * srcs_dense[rels, src]
        vrps = jnp.zeros((vfts.shape[0], D_OUT), dtype=vfts.dtype)
        vrps = vrps.at[dst].add(srcs)
        dsts = vfts @ update
        vrps = vrps.at[dst].add(dsts[dst])
        return jax.nn.relu(vrps)

    def _L3_gnn_ref(x, edge_index, W, b):
        import jax, jax.numpy as jnp
        import numpy as np
        N_NODES = 3125
        N_EDGES = 40000
        IN_CH = 128
        OUT_CH = 128
        row, col = (edge_index[0], edge_index[1])
        num_nodes = x.shape[0]
        deg = jax.ops.segment_sum(jnp.ones(row.shape[0], dtype=x.dtype), row, num_segments=num_nodes)
        deg = jnp.maximum(deg, 1.0)
        agg = jax.ops.segment_sum(x[col], row, num_segments=num_nodes)
        agg = agg / deg[:, None]
        return (x + agg) @ W.T + b
    edge_index = jnp.stack([src, dst])
    h = jnp.maximum(_layernorm(x, axis=-1), 0.0)
    x = x + _L0_gnn_ref(h, src, dst, edge_weight, L0_gnn_eps)
    h = jnp.maximum(_layernorm(x, axis=-1), 0.0)
    x = x + _L1_gnn_ref(h, edge_index, edge_attr_64, edge_attr_64_n2, L1_gnn_W_node, L1_gnn_b_node, L1_gnn_conv_weight, L1_gnn_w_ih, L1_gnn_w_hh, L1_gnn_b_ih, L1_gnn_b_hh)
    h = jnp.maximum(_layernorm(x, axis=-1), 0.0)
    x = x + _L2_gnn_ref(h, edge_index, edge_type_16, edge_attr_32, edge_attr_32_n2, L2_gnn_weight, L2_gnn_comp, L2_gnn_attn_w1, L2_gnn_attn_b1, L2_gnn_attn_w2, L2_gnn_attn_b2, L2_gnn_update)
    h = jnp.maximum(_layernorm(x, axis=-1), 0.0)
    x = x + _L3_gnn_ref(h, edge_index, L3_gnn_W, L3_gnn_b)
    return x

_drawn_inputs = setup_inputs


def setup_inputs(seed=0):
    import zlib

    import numpy as np

    out = dict(_drawn_inputs(seed))
    spreads = {'L2_gnn_attn_b1': (0.0, 0.8)}
    factors = {'edge_attr_32': 8.0,
     'edge_attr_32_n2': 8.0,
     'L1_gnn_b_hh': 3.181,
     'L2_gnn_weight': 4.975,
     'L2_gnn_comp': 4.73,
     'L2_gnn_attn_w1': 8.0,
     'L2_gnn_attn_w2': 8.0,
     'L3_gnn_b': 8.0}
    for name, (base, spread) in spreads.items():
        noise = np.random.default_rng([zlib.crc32(name.encode()), seed]).standard_normal(out[name].shape)
        drawn = base * np.exp(spread * noise) if base else spread * noise
        out[name] = jnp.asarray(drawn.astype(out[name].dtype))
    for name, factor in factors.items():
        out[name] = (out[name] * factor).astype(out[name].dtype)
    return out
```

```python
from contextlib import ExitStack

import concourse.bass as bass
from concourse import mybir

ALU = mybir.AluOpType
ACT = mybir.ActivationFunctionType
AX = mybir.AxisListType
F32 = mybir.dt.float32
BF16 = mybir.dt.bfloat16
I32 = mybir.dt.int32
U32 = mybir.dt.uint32

P = 128
D = 128
N = 6250
E = 100000
GN = 4
NG = -(-N // (P * GN))
NT = NG * GN
NP = NT * P
U = 16
HU = U // 2
ET = -(-E // (P * U)) * U
NR = ET // U
EP = ET * P
TB = 112
NB = ET // TB
ZROW = EP
PAD_KEY = NP - 1
R, B = 16, 8
LAYERS = 3
EW_P, EW_C = 80, 25
EW_N = E // EW_P
EW_CHUNKS = EW_N // EW_C
DE, DA = 64, 32
NN_FULL = N // P
N_REST = N - NN_FULL * P
BANK = 512
LN_EPS = 1e-5

PASS_L0, PASS_L1, PASS_L2, PASS_L3 = 0, 1, 1 + LAYERS, 2 + LAYERS
PREP_AT = 8
SCATTER_ROUNDS = (12, 12, NR - 24)


def gnn_kernel(nc, a, out):
    with ExitStack() as ctx:
        def sb(name, shape, dt=F32):
            return ctx.enter_context(nc.sbuf_tensor(name, shape, dt))

        def sem(name):
            return ctx.enter_context(nc.semaphore(name))

        def dram(name, shape, dt=F32):
            return nc.dram_tensor(name, shape, dt, kind="Internal").ap()

        h_rows = dram("h_rows", (NP, D))
        t_rows = dram("t_rows", (NP * R, D))
        seg_rows = dram("seg_rows", (EP + P, D))
        rank_flat = [dram(f"rank_flat_{side}", (P * ET, 1)) for side in ("dst", "src")]
        ew_flat = dram("ew_flat", (E,))
        by_src = dram("by_src", (EP, 2), U32)

        ps = ctx.enter_context(nc.psum_tensor("ps", [P, 8, BANK], F32))
        two = ps[:, :, :].rearrange("p (k b) c -> p k (b c)", b=2)

        irow = sb("irow", [P, P])
        irow_b = sb("irow_b", [P, P], BF16)
        icol = sb("icol", [P, 1])
        cols = sb("cols", [P, 6])
        ident = sb("ident", [P, P])
        ident_b = sb("ident_b", [P, P], BF16)
        before = sb("before", [P, P])
        upto = sb("upto", [P, P])
        shift = sb("shift", [P, P])
        last_to_0 = sb("last_to_0", [P, P])
        from_last = sb("from_last", [P, P])
        from_0 = sb("from_0", [P, P])
        ones = sb("ones", [P, P])
        zf = sb("zf", [P, P])
        zb = zf[:, 0:P // 2].bitcast(BF16)

        X = sb("X", [P, NT, D])
        HN = sb("HN", [P, NT, D])
        HT = sb("HT", [P, NP])
        AG = sb("AG", [P, GN, D])
        HG = sb("HG", [P, GN, D])
        HS = sb("HS", [P, GN, D])
        aT = sb("aT", [P, GN * P])
        rS = sb("rS", [P, GN * P])
        zS = sb("zS", [P, GN * P])
        nS = sb("nS", [P, GN * P])
        tS = sb("tS", [P, GN * P])
        bst = sb("bst", [P, GN, 6])
        mv = sb("mv", [P, GN, 2])
        var_e = sb("var_e", [P, NT])
        nmean = sb("nmean", [P, NT])
        rstd = sb("rstd", [P, NT])
        nbias = sb("nbias", [P, NT])
        mhalf = sb("mhalf", [P, GN])

        G = sb("G", [P, U, D])
        M = sb("M", [P, U, P])
        PR = sb("PR", [P, U, D])
        dS = PR[:, 0:GN, :].rearrange("p j d -> p (j d)")
        ixr = sb("ixr", [P, U], U32)
        crr = sb("crr", [P, U])
        nix = sb("nix", [P, GN], U32)
        six = sb("six", [P, U], U32)
        spay = sb("spay", [P, U, 2], U32)

        raw = sb("raw", [P, 4 * NB * P])
        raw4 = raw[0:TB, :].rearrange("p (k b c) -> p k b c", k=4, c=P)
        raw4_i = raw[0:TB, :].bitcast(I32).rearrange("p (k b c) -> p k b c", k=4, c=P)
        raw_pair = raw[0:TB, 0:2 * NB * P].bitcast(U32).rearrange("p (b c k) -> p b c k", b=NB, k=2)
        za = raw[0:EW_P, 0:2 * EW_C * DE].rearrange("p (k c d) -> p k c d", k=2, d=DE)
        w_f = sb("w_f", [P, ET])
        s_lo = sb("s_lo", [P, ET])
        s_hi = sb("s_hi", [P, ET])
        d_lo = sb("d_lo", [P, ET])
        d_hi = sb("d_hi", [P, ET])
        rank_d = sb("rank_d", [P, ET])
        carry_d = sb("carry_d", [P, ET])
        rank_s, carry_s = s_lo, s_hi
        ix_src = sb("ix_src", [P, ET], U32)
        ix_dst = sb("ix_dst", [P, ET], U32)
        ix_t = sb("ix_t", [P, ET], U32)
        ix_q = ix_src
        pos = sb("pos", [P, ET], U32)
        hn = HN[:, :, :].rearrange("p t d -> p (t d)")
        tab = [hn[:, k * ET:(k + 1) * ET] for k in range(4)]
        src_f, dst_f, typ_f, tmp = tab
        tmp_i = hn[:, 4 * ET:5 * ET].bitcast(I32)
        flt0 = 5 * ET
        flt = [hn[0:TB, flt0 + k * NB * P:flt0 + (k + 1) * NB * P].rearrange("p (b c) -> p b c", c=P)
               for k in range(3)]
        n_d = sb("n_d", [P, NT])
        n_s = sb("n_s", [P, NT])
        base = sb("base", [P, 2, NT])
        fin = sb("fin", [P, 2, NT], U32)
        inv_s = sb("inv_s", [P, NT])
        small = nS[:, 0:4 * NT].rearrange("p (k t) -> p k t", t=NT)
        small_i = tS[:, 0:3 * NT].bitcast(I32).rearrange("p (k t) -> p k t", t=NT)
        last_e = sb("last_e", [P, 2, NT])
        end_ix = sb("end_ix", [P, 2, NT], U32)
        rank_end = sb("rank_end", [P, 2, NT])
        tot = sb("tot", [NT, 2])
        tot_b = sb("tot_b", [NT, 2, P])

        lo_b = sb("lo_b", [P, 4, P], BF16)
        hi_b = sb("hi_b", [P, 8, NT], BF16)
        loT = sb("loT", [P, 4, P])
        run_s = sb("run_s", [P, 4, NT])
        eqm = sb("eqm", [P, 4, P], BF16)
        junk = sb("junk", [P, NT])
        note = sb("note", [P, 16])
        posr = sb("posr", [P, U])

        ew_t = HT[0:EW_P, 0:EW_N]
        t_buf = [x[:, :, :].rearrange("p u c -> p (u c)") for x in (M, G)]
        ew_r = sb("ew_r", [EW_P, EW_C])

        w_node = sb("w_node", [P, D])
        b_node = sb("b_node", [P, 1])
        eps_c = sb("eps_c", [P, 1])
        eps1 = sb("eps1", [P, 1])
        big = sb("big", [P, R * D])
        conv_raw = big[:, 0:LAYERS * D].rearrange("p (l d) -> p l d", l=LAYERS)
        ih_raw = big[:, 3 * D:6 * D].rearrange("p (l d) -> p l d", l=3)
        hh_raw = big[:, 6 * D:9 * D].rearrange("p (l d) -> p l d", l=3)
        l3_raw = big[:, 9 * D:10 * D]
        convT = big[:, 10 * D:13 * D].rearrange("p (l d) -> p l d", l=LAYERS)
        ihT = big[:, 13 * D:16 * D]
        hhT = sb("hhT", [P, 3 * D])
        wc = sb("wc", [P, LAYERS, 3 * D])
        b_ih = sb("b_ih", [P, 3])
        b_hh = sb("b_hh", [P, 3])
        b_rz = sb("b_rz", [P, 2])
        basis = sb("basis", [P, B, D])
        comp_b = sb("comp_b", [P, R * B])
        upd = sb("upd", [P, D])
        w3T = sb("w3T", [P, D])
        b3 = sb("b3", [P, D])
        erps = sb("erps", [R, 2 * D + 2 * DA])
        eix = sb("eix", [R, 2], I32)
        eix_u = sb("eix_u", [R, 2], U32)
        erT = sb("erT", [P, 3, R])
        aw1 = sb("aw1", [P, 3, D])
        ab1 = sb("ab1", [R, D])
        aw2 = sb("aw2", [R, D])
        ab2 = sb("ab2", [R, 1])
        ahid = tS[0:R, 0:2 * D].rearrange("p (k d) -> p k d", k=2)
        alog = sb("alog", [R, 2])
        adiag = sb("adiag", [R, R])
        alpha = sb("alpha", [P, R])

        s_iota = sem("s_iota")
        s_v = sem("s_v")
        s_v0 = sem("s_v0")
        s_v2 = sem("s_v2")
        s_v1 = sem("s_v1")
        s_pad = sem("s_pad")
        s_meta = [sem(f"s_meta{k}") for k in range(4)]
        s_x = sem("s_x")
        s_w = sem("s_w")
        s_rdy = sem("s_rdy")
        s_tr = sem("s_tr")
        s_dsm = sem("s_dsm")
        s_sm = sem("s_sm")
        s_eix = sem("s_eix")
        s_eg = [sem("s_eg0"), sem("s_eg1"), sem("s_eg2")]
        s_tab = sem("s_tab")
        s_ewl = sem("s_ewl")
        s_ewc = sem("s_ewc")
        s_att = sem("s_att")
        s_idx = sem("s_idx")
        s_m = sem("s_m")
        s_g = [sem(f"s_g{u}") for u in range(U)]
        s_done = sem("s_done")
        s_pc = sem("s_pc")
        s_ps = [sem("s_ps0"), sem("s_ps1")]
        s_oh = sem("s_oh")
        s_cnt = sem("s_cnt")
        s_loT = sem("s_loT")
        s_lc = sem("s_lc")
        s_eq = sem("s_eq")
        s_eqm = sem("s_eqm")
        s_pp = sem("s_pp")
        s_pos = sem("s_pos")
        s_posw = sem("s_posw")
        s_sct = [sem("s_sct0"), sem("s_sct1")]
        s_scp = sem("s_scp")
        s_nx = sem("s_nx")
        s_hold = [sem(f"s_hold{k}") for k in range(3)]
        s_ag = [sem(f"s_ag{j}") for j in range(GN)]
        s_var = sem("s_var")
        s_rs = sem("s_rs")
        s_ln = sem("s_ln")
        s_hg = sem("s_hg")
        s_hst = sem("s_hst")
        s_a1 = sem("s_a1")
        s_a2 = sem("s_a2")
        s_a3 = sem("s_a3")
        s_a4 = sem("s_a4")
        s_a5 = sem("s_a5")
        s_a6 = sem("s_a6")
        s_a7 = sem("s_a7")
        s_a8 = sem("s_a8")
        s_a9 = sem("s_a9")
        s_a10 = sem("s_a10")
        s_te = [sem("s_te0"), sem("s_te1")]
        s_ts = [sem("s_ts0"), sem("s_ts1")]
        s_th = sem("s_th")
        s_tm = sem("s_tm")

        LN0, N0, G0, G1, G2, N2, N3 = range(7)
        per = {
            "ag": (0, 1, 1, 1, 1, 1, 1),
            "ln": (1, 1, 0, 0, 1, 1, 0),
            "a1": (0, 1, 1, 1, 1, 0, 1),
            "a3": (0, 1, 3, 3, 3, 1, 1),
            "a4": (0, 1, 3, 3, 3, 0, 0),
            "a5": (0, 1, 1, 1, 1, 0, 0),
            "a6": (0, 1, 1, 1, 0, 0, 1),
            "a7": (0, 1, 0, 0, 1, 1, 1),
            "a8": (0, 0, 2, 2, 2, 0, 1),
            "a2": (0, 1, 1, 1, 1, 1, 1),
            "a10": (0, 1, 1, 1, 1, 0, 0),
            "a9": (0, 0, 0, 0, 1, 0, 0),
            "hst": (1, 1, 1, 1, 1, 1, 1),
        }

        def b(name, phase):
            return 1 + NG * sum(per[name][:phase])

        def stores(phase):
            return b("hst", phase)

        def staged(eng, stages):
            deep = max(lag for lag, _ in stages)
            for s in range(deep):
                for lag, step in stages:
                    if s >= lag:
                        step(s - lag)
            with eng.Fori(deep, NG) as s:
                for lag, step in stages:
                    step(s - lag)
            for s in range(NG, NG + deep):
                for lag, step in stages:
                    if s - lag < NG:
                        step(s - lag)

        def group(t, g):
            return t[:, bass.ds(g * GN, GN), :]

        def feat(g):
            return HT[:, bass.ds(g * GN * P, GN * P)]

        def bank(k, n=GN * P):
            return ps[:, k, 0:n]

        def quarters(k):
            return ps[:, k, :].rearrange("p (j d) -> p j d", j=GN)

        N_LOADS = 26
        block = ctx.enter_context(nc.Block())
        rows_of = h_rows.rearrange("(t p) d -> p t d", p=P)
        WHOLE = (E // P) // TB * TB * P
        ROWS = E // P - WHOLE // P
        REST = E - WHOLE - ROWS * P
        T0 = 4 * TB

        @block.sync
        def _(sp):
            def tile_load(dst, k, flat):
                sp.dma_start(dst[:, k, 0:NB - 1, :], flat[0:WHOLE].rearrange("(b p c) -> p b c", p=TB, c=P)) \
                    .then_inc(s_meta[k], 16)
                sp.dma_start(dst[0:ROWS, k, NB - 1, :], flat[WHOLE:E - REST].rearrange("(p c) -> p c", c=P)) \
                    .then_inc(s_meta[k], 16)
                sp.dma_start(dst[ROWS:ROWS + 1, k, NB - 1, 0:REST],
                             flat[E - REST:E].rearrange("(p c) -> p c", p=1)).then_inc(s_meta[k], 16)

            for s in (s_hst, *s_ps, *s_ts):
                sp.sem_inc(s, 16)
            sp.wait_ge(s_pad, 1)
            for k, name in enumerate(("src", "dst", "edge_type_16", "edge_weight")):
                tile_load(raw4_i if k < 3 else raw4, k, a[name])
            sp.dma_start(X[:, 0:NN_FULL, :], a["x"][0:NN_FULL * P].rearrange("(t p) d -> p t d", p=P)) \
                .then_inc(s_x, 16)
            sp.dma_start(X[0:N_REST, NN_FULL, :], a["x"][NN_FULL * P:N]).then_inc(s_x, 16)

            def load(dst, src):
                sp.dma_start(dst, src).then_inc(s_w, 16)

            def row(v, n):
                return v.rearrange("(a o) -> a o", a=1).broadcast_to((n, v.shape[0]))

            load(eps_c[:], row(a["L0_gnn_eps"], P))
            load(w_node[:], a["L1_gnn_W_node"])
            load(b_node[:], a["L1_gnn_b_node"].rearrange("(p c) -> p c", c=1))
            load(conv_raw, a["L1_gnn_conv_weight"].rearrange("l i o -> i l o"))
            load(ih_raw, a["L1_gnn_w_ih"].rearrange("(g o) i -> o g i", g=3))
            load(hh_raw, a["L1_gnn_w_hh"].rearrange("(g o) i -> o g i", g=3))
            for g in range(3):
                load(b_ih[:, g:g + 1], a["L1_gnn_b_ih"][g * D:(g + 1) * D].rearrange("(p c) -> p c", c=1))
                load(b_hh[:, g:g + 1], a["L1_gnn_b_hh"][g * D:(g + 1) * D].rearrange("(p c) -> p c", c=1))
            load(basis[:], a["L2_gnn_weight"].rearrange("b i o -> i b o"))
            load(comp_b[:, :], row(a["L2_gnn_comp"].rearrange("r b -> (r b)"), P))
            load(upd[:], a["L2_gnn_update"])
            load(l3_raw, a["L3_gnn_W"])
            load(b3[:], row(a["L3_gnn_b"], P))
            load(erps[:, 2 * D:2 * D + DA], a["edge_attr_32"][0:R])
            load(erps[:, 2 * D + DA:2 * D + 2 * DA], a["edge_attr_32_n2"][0:R])
            load(eix[:, 0:1], a["src"][0:R].rearrange("(p c) -> p c", c=1))
            load(eix[:, 1:2], a["dst"][0:R].rearrange("(p c) -> p c", c=1))
            load(aw1[:, 0:2, :], a["L2_gnn_attn_w1"][0:2 * D].rearrange("(c p) o -> p c o", p=P))
            load(aw1[0:2 * DA, 2, :], a["L2_gnn_attn_w1"][2 * D:2 * D + 2 * DA])
            load(ab1[:], row(a["L2_gnn_attn_b1"], R))
            load(aw2[:], row(a["L2_gnn_attn_w2"].rearrange("o a -> (o a)"), R))
            load(ab2[:], row(a["L2_gnn_attn_b2"], R))
            sp.dma_start(seg_rows[EP:EP + P], zf[:]).then_inc(s_dsm, 16)
            sp.wait_ge(s_sm, 1)
            sp.dma_start(rank_flat[0].rearrange("(p t) c -> p (t c)", p=P), rank_d[:]).then_inc(s_dsm, 16)

            z_dram = a["edge_attr_64_n2"].rearrange("(p c) d -> p c d", p=EW_P)
            e_dram = a["edge_attr_64"].rearrange("(p c) d -> p c d", p=EW_P)

            def ew_load(c):
                sp.dma_start(za[:, 0, :, :], z_dram[:, bass.ds(c * EW_C, EW_C), :]).then_inc(s_ewl, 16)
                sp.dma_start(za[:, 1, :, :], e_dram[:, bass.ds(c * EW_C, EW_C), :]).then_inc(s_ewl, 16)

            ew_load(0)
            with sp.Fori(0, NG) as i:
                sp.wait_ge(s_hg, b("ln", LN0) + i + 1)
                sp.dma_start(rows_of[:, bass.ds(i * GN, GN), :], group(HN, i)).then_inc(s_hst, 16)

            segs = seg_rows[0:EP].rearrange("(t p) d -> p t d", p=P)

            def seg_store(k, i, q):
                sp.wait_ge(s_pc, 4 + k * ET + i * U + (q + 1) * HU)
                sp.dma_start(segs[:, bass.ds(i * U + q * HU, HU), :], PR[:, q * HU:(q + 1) * HU, :]) \
                    .then_inc(s_ps[q], 16)

            def h_store(phase, src, ready, at):
                with sp.Fori(0, NG) as i:
                    sp.wait_ge(ready, i + at + 1)
                    sp.dma_start(rows_of[:, bass.ds(i * GN, GN), :], src(i)).then_inc(s_hst, 16)

            with sp.Fori(0, NR) as i:
                sp.wait_ge(s_ewc, i + 1)
                ew_load(i + 1)
                seg_store(PASS_L0, i, 0)
                seg_store(PASS_L0, i, 1)
            sp.wait_ge(s_sm, 2)
            sp.dma_start(ew_flat.rearrange("(p c) -> p c", p=EW_P), ew_t).then_inc(s_dsm, 16)
            sp.wait_ge(s_dsm, 48)
            tile_load(raw4, 3, ew_flat)
            h_store(N0, lambda i: HS[:], s_a6, b("a6", N0))
            for l in range(LAYERS):
                with sp.Fori(0, NR) as i:
                    seg_store(PASS_L1 + l, i, 0)
                    seg_store(PASS_L1 + l, i, 1)
                if l < LAYERS - 1:
                    h_store(G0 + l, lambda i: HS[:], s_a6, b("a6", G0 + l))
                else:
                    h_store(G0 + l, lambda i: HG[:], s_hg, b("ln", G0 + l))
            t_out = t_rows.rearrange("(t p r) d -> p t (r d)", p=P, r=R)
            with sp.Fori(0, NT // 2) as i:
                for q in range(2):
                    for h in range(2):
                        sp.wait_ge(s_te[h], 1 + i * 2 + q + 1)
                    sp.dma_start(t_out[:, bass.ds(2 * i + q, 1), :].rearrange("p t c -> p (t c)"), t_buf[q]) \
                        .then_inc(s_ts[q], 16)
            for q in range(2):
                sp.wait_ge(s_sct[q], 16 * HU * NR)
            sp.dma_start(raw_pair.rearrange("p b c k -> p b (c k)"),
                         by_src.rearrange("(b p c) k -> p b (c k)", p=TB, c=P)).then_inc(s_meta[0], 16)
            with sp.Fori(0, PREP_AT) as i:
                seg_store(PASS_L2, i, 0)
                seg_store(PASS_L2, i, 1)
            sp.wait_ge(s_sm, 3)
            sp.dma_start(rank_flat[1].rearrange("(p t) c -> p (t c)", p=P), rank_s[:]).then_inc(s_dsm, 16)
            with sp.Fori(PREP_AT, NR) as i:
                seg_store(PASS_L2, i, 0)
                seg_store(PASS_L2, i, 1)
            h_store(N2, lambda i: group(HN, i), s_hg, b("ln", N2))
            with sp.Fori(0, NR) as i:
                seg_store(PASS_L3, i, 0)
                seg_store(PASS_L3, i, 1)
            out_of = out[0:NN_FULL * P].rearrange("(t p) d -> p t d", p=P)
            with sp.Fori(0, NG - 1) as i:
                sp.wait_ge(s_a6, b("a6", N3) + i + 1)
                sp.dma_start(out_of[:, bass.ds(i * GN, GN), :], HS[:]).then_inc(s_hst, 16)
            sp.wait_ge(s_a6, b("a6", N3) + NG)
            sp.dma_start(out[NN_FULL * P:N], HS[0:N_REST, NN_FULL - (NG - 1) * GN, :]).then_inc(s_hst, 16)
            sp.wait_ge(s_hst, 16 * (stores(N3) + NG))

        @block.gpsimd
        def _(pool):
            def hold(s, value):
                pool.wait_ge(s, value)
                pool.sem_inc(s_hold[0], 1)

            for s in (s_rs, s_ln, s_nx):
                pool.sem_inc(s, 1)
            nc.gpsimd.iota(irow[:], [[1, P]], base=0, channel_multiplier=0,
                           allow_small_or_imprecise_dtypes=True)
            nc.gpsimd.iota(icol[:], [[0, 1]], base=0, channel_multiplier=1,
                           allow_small_or_imprecise_dtypes=True).then_inc(s_iota, 1)

            def gather_pass(k, r0, r1, table):
                with pool.Fori(r0, r1) as i:
                    for q in range(2):
                        hold(s_idx, 2 * (k * NR + i) + q + 1)
                        for u in range(q * HU, (q + 1) * HU):
                            nc.gpsimd.indirect_dma_start(
                                G[:, u, :], None, table,
                                bass.IndirectOffsetOnAxis(ap=ixr[:, u:u + 1], axis=0)).then_inc(s_g[u], 16)

            def deviation(phase):
                def step(i):
                    at = bass.ds(i * GN, GN)
                    hold(s_var, b("ln", phase) + i + 1)
                    nc.gpsimd.tensor_tensor(rstd[:, at], var_e[:, at], mhalf[:], ALU.pow).then_inc(s_rs, 1)
                    hold(s_rs, b("ln", phase) + i + 1)
                    nc.gpsimd.tensor_tensor(nbias[:, at], nmean[:, at], rstd[:, at], ALU.mult).then_inc(s_ln, 1)
                return step

            def node_gather(phase, k, side, used, at):
                pool.wait_ge(s_ps[0], 16 * (1 + NR * (k + 1)))
                pool.wait_ge(s_ps[1], 16 * (1 + NR * (k + 1)))
                pool.wait_ge(s_dsm, 32)
                pool.wait_ge(s_tab, side + 1)

                def gather(i):
                    hold(used, at + i)
                    nc.gpsimd.tensor_copy(nix[:], fin[:, side, bass.ds(i * GN, GN)]).then_inc(s_nx, 1)
                    hold(s_nx, b("ag", phase) + i + 1)
                    for j in range(GN):
                        nc.gpsimd.indirect_dma_start(
                            AG[:, j, :], None, seg_rows,
                            bass.IndirectOffsetOnAxis(ap=nix[:, j:j + 1], axis=0)).then_inc(s_ag[j], 16)

                staged(pool, [(0, gather)] + ([(1, deviation(phase))] if per["ln"][phase] else []))

            def rank_gather(side):
                pool.wait_ge(s_eix, side + 1)
                pool.wait_ge(s_dsm, (32, 64)[side])
                for t in range(NT):
                    nc.gpsimd.indirect_dma_start(
                        rank_end[:, side, t:t + 1], None, rank_flat[side],
                        bass.IndirectOffsetOnAxis(ap=end_ix[:, side, t:t + 1], axis=0)) \
                        .then_inc(s_eg[side], 16)

            def scatter(r0, r1):
                def round_of(i):
                    for q in range(2):
                        lo = q * HU
                        if not (isinstance(i, int) and i == 0):
                            hold(s_sct[q], 16 * HU * i)
                        at = bass.ds(i * U + lo, HU)
                        nc.gpsimd.tensor_copy(six[:, lo:lo + HU], pos[:, at])
                        nc.gpsimd.tensor_copy(spay[:, lo:lo + HU, 0], ix_src[:, at])
                        nc.gpsimd.tensor_copy(spay[:, lo:lo + HU, 1], ix_dst[:, at]).then_inc(s_scp, 1)
                        hold(s_scp, 2 * i + q + 1)
                        for u in range(lo, lo + HU):
                            nc.gpsimd.indirect_dma_start(
                                by_src, bass.IndirectOffsetOnAxis(ap=six[:, u:u + 1], axis=0),
                                spay[:, u, :], None).then_inc(s_sct[q], 16)

                if r0 == 0:
                    round_of(0)
                with pool.Fori(max(r0, 1), r1) as i:
                    round_of(i)

            with pool.Fori(0, NG) as i:
                deviation(LN0)(i)
            pool.wait_ge(s_hst, 16 * stores(N0))
            gather_pass(PASS_L0, 0, NR, h_rows)
            rank_gather(0)
            node_gather(N0, PASS_L0, 0, s_a7, b("a7", N0))
            at = 0
            for l in range(LAYERS):
                pool.wait_ge(s_hst, 16 * stores(G0 + l))
                gather_pass(PASS_L1 + l, 0, NR, h_rows)
                node_gather(G0 + l, PASS_L1 + l, 0, s_a1, b("a1", G0 + l))
                if l == 0:
                    pool.wait_ge(s_posw, NR)
                if l == LAYERS - 1:
                    pool.wait_ge(s_hst, 16 * b("hst", N2))
                    pool.wait_ge(s_eix, 2)
                    for c in range(2):
                        nc.gpsimd.indirect_dma_start(
                            erps[:, c * D:(c + 1) * D], None, h_rows,
                            bass.IndirectOffsetOnAxis(ap=eix_u[:, c:c + 1], axis=0)).then_inc(s_eg[2], 16)
                scatter(at, at + SCATTER_ROUNDS[l])
                at += SCATTER_ROUNDS[l]
            for q in range(2):
                pool.wait_ge(s_ts[q], 16 * (1 + NT // 2))
            gather_pass(PASS_L2, 0, PREP_AT + 1, t_rows)
            rank_gather(1)
            gather_pass(PASS_L2, PREP_AT + 1, NR, t_rows)
            node_gather(N2, PASS_L2, 0, s_a7, b("a7", N2))
            pool.wait_ge(s_hst, 16 * stores(N3))
            gather_pass(PASS_L3, 0, NR, h_rows)
            node_gather(N3, PASS_L3, 1, s_a7, b("a7", N3))

        @block.tensor
        def _(pe):
            units = [0]

            def unit():
                units[0] += 1
                pe.wait_ge(s_rdy, units[0])

            def mm(dst, lhsT, rhs, start=True, stop=True):
                return nc.tensor.matmul(dst, lhsT, rhs, start=start, stop=stop, skip_group_check=True)

            def by_edge(k, tiles):
                unit()
                for c in range(NB):
                    at = c * TB if c < 4 else BANK + (c - 4) * TB
                    last = nc.tensor.transpose(two[:, k, at:at + TB], tiles[:, c, :], ident[0:TB, 0:TB])
                last.then_inc(s_tr, 1)

            def over(k, lhsT, rhs):
                mm(two[:, k, 0:BANK], lhsT, rhs[:, 0:BANK])
                return mm(two[:, k, BANK:ET], lhsT, rhs[:, BANK:ET])

            def previous_keys(k, keys):
                unit()
                mm(two[:, k, 0:BANK], shift[:], keys[:, 0:BANK], stop=False)
                mm(two[:, k, 1:BANK], last_to_0[:], keys[:, 0:BANK - 1], start=False)
                mm(two[:, k, BANK:ET], shift[:], keys[:, BANK:ET], stop=False)
                mm(two[:, k, BANK:ET], last_to_0[:], keys[:, BANK - 1:ET - 1], start=False).then_inc(s_tr, 1)

            def segment_units(k0, k1, keys, fresh, same, rank):
                previous_keys(k0, keys)
                unit()
                over(k1, upto[:], fresh).then_inc(s_tr, 1)
                unit()
                over(k0, from_0[:], same)
                over(k1, from_last[:], rank).then_inc(s_tr, 1)

            pe.sem_inc(s_done, U)
            pe.sem_inc(s_cnt, 2)
            for s in (s_a1, s_a3, s_a5, s_a9, s_eq):
                pe.sem_inc(s, 1)
            for k in range(3):
                by_edge(k, flt[k])
            by_edge(3, raw4[:, 3])
            unit()
            for l in range(LAYERS):
                nc.tensor.transpose(ps[:, 0, l * D:(l + 1) * D], conv_raw[:, l, :], ident[:])
                nc.tensor.transpose(ps[:, 1, l * D:(l + 1) * D], ih_raw[:, l, :], ident[:])
                nc.tensor.transpose(ps[:, 2, l * D:(l + 1) * D], hh_raw[:, l, :], ident[:])
            nc.tensor.transpose(ps[:, 3, 0:D], l3_raw, ident[:]).then_inc(s_tr, 1)
            unit()
            for l in range(LAYERS):
                last = mm(ps[:, 4 + l, 0:3 * D], convT[:, l, :], ihT)
            last.then_inc(s_tr, 1)
            segment_units(2, 3, dst_f, tab[3], carry_d, rank_d)
            unit()
            mm(ps[:, 6, 0:NT], zb, zb[:, 0:NT])
            mm(ps[:, 7, 0:NT], zb, zb[:, 0:NT]).then_inc(s_tr, 1)

            def gather_pass(k, r0, r1, extra=None, drain=0):
                with pe.Fori(r0, r1) as i:
                    for u in range(U):
                        t = i * U + u
                        pe.wait_ge(s_m, k * ET + t + 1)
                        pe.wait_ge(s_g[u], 16 * (k * NR + i + 1))
                        mm(ps[:, u % 4, 0:D], M[:, u, :], G[:, u, :], stop=False)
                        pe.wait_ge(s_pc, k * ET + t + 4)
                        mm(ps[0:1, u % 4, 0:D], crr[:, u:u + 1], PR[:, (u - 1) % U, :],
                           start=False).then_inc(s_done, 1)
                        if extra:
                            extra(i, u)
                    for u in range(U, U + drain):
                        extra(i, u)

            def count(i, u):
                pe.wait_ge(s_oh, i * U + u + 1)
                q = 2 * (u % 2)
                mm(ps[:, 6, 0:NT], lo_b[:, q, :], hi_b[:, q, :], start=False)
                mm(ps[:, 7, 0:NT], lo_b[:, q + 1, :], hi_b[:, q + 1, :], start=False).then_inc(s_cnt, 1)

            def place(i, u):
                if u < U:
                    t = i * U + u
                    pe.wait_ge(s_oh, ET + t + 1)
                    pe.wait_ge(s_lc, 1 + t)
                    nc.tensor.transpose(ps[:, 4, 0:P // 2].bitcast(BF16), lo_b[:, u % 4, :], ident_b[:]) \
                        .then_inc(s_loT, 1)
                if 1 <= u <= U:
                    v = u - 1
                    t = i * U + v
                    pe.wait_ge(s_lc, 1 + t + 1)
                    if v >= 1:
                        pe.wait_ge(s_eqm, t)
                    mm(ps[:, 7, 0:P], loT[:, v % 4, :], loT[:, v % 4, :])
                    mm(ps[:, 6, 0:NT], lo_b[:, v % 4, :], hi_b[:, v % 8, :], start=False).then_inc(s_eq, 1)
                if 3 <= u < U + 3:
                    v = u - 3
                    t = i * U + v
                    pe.wait_ge(s_eqm, t + 1)
                    if v >= 1:
                        pe.wait_ge(s_pos, 1 + t)
                    mm(ps[:, 5, 0:NT], loT[:, v % 4, :], run_s[:, v % 4, :], stop=False)
                    mm(ps[:, 5, 0:NT], eqm[:, v % 4, :], hi_b[:, v % 8, :], start=False) \
                        .then_inc(s_pp, 1)

            def totals(side, counts, to):
                unit()
                mm(ps[0:NT, 4, 0:1], counts[:], ones[:, 0:1]).then_inc(s_tr, 1)
                unit()
                mm(ps[:, to, 0:NT], before[:], counts[:], stop=False)
                mm(ps[:, to, 0:NT], tot_b[:, side, :], before[0:NT, 0:NT], start=False).then_inc(s_tr, 1)

            def turn(dst, src, done, rows=False):
                for j in range(GN):
                    last = nc.tensor.transpose(ps[:, dst, j * P:(j + 1) * P], src(j), ident[:])
                last.then_inc(done, 1)

            def new_h(j):
                return dS[:, j * P:(j + 1) * P]

            def wait_group(phase, i):
                for j in range(GN):
                    pe.wait_ge(s_ag[j], 16 * (b("ag", phase) + i))

            gather_pass(PASS_L0, 0, NR, count)
            totals(0, n_d, 5)
            totals(1, n_s, 6)
            by_edge(1, raw4[:, 3])

            def n0_in(i):
                pe.wait_ge(s_hg, b("ln", N0) + i + 1)
                pe.wait_ge(s_a2, b("a2", N0) + i)
                turn(4, lambda j: HG[:, j, :], s_a1)

            def n0_mm(i):
                pe.wait_ge(s_a2, b("a2", N0) + i + 1)
                pe.wait_ge(s_a10, b("a10", N0) + i)
                mm(bank(0), w_node[:], aT[:]).then_inc(s_a3, 1)

            def n0_back(i):
                pe.wait_ge(s_a4, b("a4", N0) + i + 1)
                pe.wait_ge(s_a6, b("a6", N0) + i)
                turn(5, new_h, s_a5)

            staged(pe, [(0, n0_in), (1, n0_mm), (2, n0_back)])

            for l in range(LAYERS):
                pe.wait_ge(s_a10, b("a10", G0 + l))
                gather_pass(PASS_L1 + l, 0, NR, place if l == 0 else None, 4 if l == 0 else 0)
                ph = G0 + l

                def gru_gates(i):
                    wait_group(ph, i)
                    pe.wait_ge(s_a2, b("a2", ph) + i)
                    turn(4, lambda j: AG[:, j, :], s_a1)
                    pe.wait_ge(s_a4, b("a4", ph) + 3 * i - 2)
                    if not (isinstance(i, int) and i == 0):
                        pe.wait_ge(s_a8, b("a8", ph) + 2 * i - 1)
                    mm(bank(0), hhT[:, 0:D], feat(i), stop=False)
                    mm(bank(3), hhT[:, 2 * D:3 * D], feat(i))
                    pe.wait_ge(s_a2, b("a2", ph) + i + 1)
                    mm(bank(0), wc[:, l, 0:D], aT[:], start=False).then_inc(s_a3, 1)
                    mm(bank(2), wc[:, l, 2 * D:3 * D], aT[:]).then_inc(s_a3, 1)
                    pe.wait_ge(s_a4, b("a4", ph) + 3 * i - 1)
                    mm(bank(1), hhT[:, D:2 * D], feat(i), stop=False)
                    mm(bank(1), wc[:, l, D:2 * D], aT[:], start=False).then_inc(s_a3, 1)

                def gru_back(i):
                    pe.wait_ge(s_a8, b("a8", ph) + 2 * i + 2)
                    if l < LAYERS - 1:
                        pe.wait_ge(s_a6, b("a6", ph) + i)
                    else:
                        pe.wait_ge(s_a7, b("a7", G2) + i)
                    turn(5, new_h, s_a5)

                def next_in(i):
                    pe.wait_ge(s_hg, b("ln", G2) + i + 1)
                    pe.wait_ge(s_a10, b("a10", G2) + i)
                    turn(6, lambda j: HG[:, j, :], s_a9)

                staged(pe, [(0, gru_gates), (1, gru_back)] + ([(2, next_in)] if l == LAYERS - 1 else []))

            unit()
            for c, w in ((0, D), (1, D), (2, 2 * DA)):
                last = nc.tensor.transpose(ps[0:w, 4, c * R:(c + 1) * R], erps[:, c * D:c * D + w],
                                           ident[0:R, 0:R])
            last.then_inc(s_tr, 1)
            unit()
            for c, w in ((0, D), (1, D), (2, 2 * DA)):
                last = mm(ps[0:R, 5, 0:D], erT[0:w, c, :], aw1[0:w, c, :], start=c == 0, stop=c == 2)
            last.then_inc(s_tr, 1)
            unit()
            mm(ps[:, 4, 64:64 + R], ones[0:R, :], adiag[:]).then_inc(s_tr, 1)
            unit()
            with pe.Fori(0, NT // 2) as i:
                for q in range(2):
                    for h in range(2):
                        pe.wait_ge(s_te[h], 1 + i * 2 + q)
                    pe.wait_ge(s_th, i * 2 + q + 1)
                    for c in range(4):
                        last = mm(bank(4 * q + c), dS[:, q * P:(q + 1) * P],
                                  big[:, c * BANK:(c + 1) * BANK])
                    last.then_inc(s_tm, 1)
            for h in range(2):
                pe.wait_ge(s_te[h], 1 + NT)
            gather_pass(PASS_L2, 0, PREP_AT)
            by_edge(2, flt[0])
            by_edge(3, flt[1])
            segment_units(2, 3, src_f, tab[3], carry_s, rank_s)
            gather_pass(PASS_L2, PREP_AT, NR)

            def n2_mm(i):
                pe.wait_ge(s_a7, b("a7", N2) + i)
                pe.wait_ge(s_a2, b("a2", N2) + i + 1)
                for j in range(GN):
                    last = mm(ps[:, 0, j * D:(j + 1) * D], aT[:, j * P:(j + 1) * P], upd[:])
                last.then_inc(s_a3, 1)

            staged(pe, [(0, n2_mm)])
            gather_pass(PASS_L3, 0, NR)

            def n3_in(i):
                pe.wait_ge(s_a8, b("a8", N3) + i + 1)
                pe.wait_ge(s_a2, b("a2", N3) + i)
                turn(4, lambda j: HG[:, j, :], s_a1)

            def n3_mm(i):
                pe.wait_ge(s_a2, b("a2", N3) + i + 1)
                pe.wait_ge(s_a6, b("a6", N3) + i)
                for j in range(GN):
                    last = mm(ps[:, 0, j * D:(j + 1) * D], aT[:, j * P:(j + 1) * P], w3T[:])
                last.then_inc(s_a3, 1)

            staged(pe, [(0, n3_in), (1, n3_mm)])

        @block.vector
        def _(dve):
            V = nc.vector

            class Chain:

                def __init__(self, s):
                    self.s, self.base, self.k, self.at = s, 0, 0, 0

                def __call__(self, ins):
                    self.k += 1
                    ins.then_inc(self.s, 1)
                    dve.wait_ge(self.s, self.at + self.base + self.k)

                def turn(self, i, steps):
                    self.k, self.at = 0, i * steps

                def leave(self, turns, steps):
                    assert self.k == steps
                    self.base, self.k, self.at = self.base + turns * steps, 0, 0

            link, first, norm = Chain(s_v), Chain(s_v0), Chain(s_v1)

            def hold(s, value):
                dve.wait_ge(s, value)
                dve.sem_inc(s_hold[1], 1)

            noted = [0]

            def signal(s):
                V.memset(note[:, noted[0]:noted[0] + 1], 0.0).then_inc(s, 1)
                noted[0] += 1

            units = [0]

            def ready(ins):
                ins.then_inc(s_rdy, 1)

            def unit_done():
                units[0] += 1
                dve.wait_ge(s_tr, units[0])

            for s in (s_var, s_a6, s_a7, s_a8, s_pos, s_te[1]):
                dve.sem_inc(s, 1)
            V.memset(raw4_i[:, 0:2, NB - 1, :], PAD_KEY)
            V.memset(raw4_i[:, 2, NB - 1, :], 0)
            V.memset(raw4[:, 3, NB - 1, :], 0.0)
            V.memset(zf[:], 0.0)
            V.memset(ones[:], 1.0)
            V.memset(mhalf[:], -0.5)
            V.memset(PR[:], 0.0)
            V.memset(X[:, NN_FULL:NT, :], 0.0).then_inc(s_pad, 1)

            dve.wait_ge(s_iota, 1)
            link(V.tensor_scalar(cols[:, 0:1], icol[:], 0.0, None, ALU.is_gt))
            V.tensor_scalar(cols[:, 1:2], icol[:], 1.0, None, ALU.add)
            V.tensor_scalar(cols[:, 2:3], icol[:], float(P - 1), None, ALU.is_equal)
            link(V.tensor_scalar(cols[:, 3:4], icol[:], 0.0, None, ALU.is_equal))
            V.tensor_copy(irow_b[:], irow[:])
            V.tensor_scalar(ident[:], irow[:], icol[:], None, ALU.is_equal)
            V.tensor_scalar(ident_b[:], irow[:], icol[:], None, ALU.is_equal)
            V.tensor_scalar(before[:], irow[:], icol[:], None, ALU.is_gt)
            V.tensor_scalar(upto[:], irow[:], icol[:], cols[:, 0:1], ALU.is_ge, ALU.mult)
            V.tensor_scalar(shift[:], irow[:], cols[:, 1:2], None, ALU.is_equal)
            V.tensor_scalar(last_to_0[:], irow[:], 0.0, cols[:, 2:3], ALU.is_equal, ALU.mult)
            V.tensor_scalar(from_last[:], ones[:], cols[:, 2:3], None, ALU.mult)
            link(V.tensor_scalar(from_0[:], ones[:], cols[:, 3:4], None, ALU.mult))

            for k in range(3):
                dve.wait_ge(s_meta[k], 48)
                ready(V.tensor_copy(flt[k], raw4_i[:, k]))
            dve.wait_ge(s_meta[3], 48)
            signal(s_rdy)

            def from_pair(dst, k):
                V.tensor_copy(dst[:, 0:T0], two[:, k, 0:T0])
                return V.tensor_copy(dst[:, T0:ET], two[:, k, BANK:BANK + ET - T0])

            for k, dst in enumerate((src_f, dst_f, typ_f, w_f[:])):
                unit_done()
                link(from_pair(dst, k))
            V.tensor_copy(ix_src[:], src_f)
            V.tensor_copy(ix_dst[:], dst_f)
            V.scalar_tensor_tensor(ix_t[:], src_f, float(R), typ_f, ALU.mult, ALU.add)
            dve.wait_ge(s_w, 16 * N_LOADS)
            signal(s_rdy)
            shifted = tmp.bitcast(I32)
            for key, lo, hi in ((src_f, s_lo, s_hi), (dst_f, d_lo, d_hi)):
                link(V.tensor_copy(tmp_i, key))
                link(V.tensor_single_scalar(shifted, tmp_i, 7, ALU.logical_shift_right))
                link(V.tensor_copy(hi[:], shifted))
                link(V.scalar_tensor_tensor(lo[:], hi[:], -float(P), key, ALU.mult, ALU.add))
            unit_done()
            V.tensor_copy(convT, ps[:, 0, 0:3 * D].rearrange("p (l d) -> p l d", l=LAYERS))
            V.tensor_copy(ihT, ps[:, 1, 0:3 * D])
            V.tensor_copy(hhT[:], ps[:, 2, 0:3 * D])
            ready(V.tensor_copy(w3T[:], ps[:, 3, 0:D]))
            unit_done()
            link(V.tensor_copy(wc[:], ps[:, 4:4 + LAYERS, 0:3 * D]))
            V.tensor_tensor(b_rz[:], b_ih[:, 0:2], b_hh[:, 0:2], ALU.add)
            V.tensor_copy(eix_u[:], eix[:])
            V.memset(ahid, 0.0)

            def segments(keys, same, rank, k0, k1, sm):
                fresh = tab[3]
                unit_done()
                V.tensor_tensor(same[:, 0:BANK], two[:, k0, 0:BANK], keys[:, 0:BANK], ALU.is_equal)
                link(V.tensor_tensor(same[:, BANK:ET], two[:, k0, BANK:ET], keys[:, BANK:ET], ALU.is_equal))
                link(V.memset(same[0:1, 0:1], 0.0))
                ready(V.tensor_scalar(fresh, same, -1.0, 1.0, ALU.mult, ALU.add))
                unit_done()
                ready(V.tensor_copy(rank, two[:, k1, 0:ET]))
                unit_done()
                link(V.tensor_copy(fresh, two[:, k0, 0:ET]))
                link(V.memset(same[:, 0:1], 0.0))
                link(V.scalar_tensor_tensor(same[:, 1:ET], two[:, k1, 0:ET - 1], icol[:], fresh[:, 1:ET],
                                            ALU.is_equal, ALU.mult))
                signal(s_sm)

            signal(s_rdy)
            segments(dst_f, carry_d[:], rank_d[:], 2, 3, s_sm)
            signal(s_rdy)
            unit_done()

            def norm_step(ph, i):
                norm.turn(i, 2)
                dve.sem_inc(s_hold[1], 1)
                for j in range(GN):
                    last = V.bn_stats(bst[:, j, :], X[:, bass.ds(i * GN + j, 1), :].rearrange("p t d -> p (t d)"))
                norm(last)
                dve.sem_inc(s_hold[1], 1)
                for j in range(GN):
                    last = V.bn_aggr(mv[:, j, :], bst[:, j, :])
                norm(last)
                V.tensor_scalar(var_e[:, bass.ds(i * GN, GN)], mv[:, :, 1], LN_EPS, None, ALU.add)
                V.tensor_scalar(nmean[:, bass.ds(i * GN, GN)], mv[:, :, 0], -1.0, None, ALU.mult) \
                    .then_inc(s_var, 1)

            dve.wait_ge(s_x, 32)
            with dve.Fori(0, NG) as i:
                norm_step(LN0, i)
            norm.leave(NG, 2)

            def ew_chunk(c, turn):
                link.turn(turn, 2)
                dve.wait_ge(s_ewl, 32 * (c + 1))
                link(V.tensor_tensor(za[:, 0, :, :], za[:, 0, :, :], za[:, 1, :, :], ALU.mult))
                link(V.tensor_reduce(ew_r[:], za[:, 0, :, :], AX.X, ALU.add))
                V.tensor_copy(ew_t[:, bass.ds(c * EW_C, EW_C)], ew_r[:]).then_inc(s_ewc, 1)

            link.leave(1, link.k)
            ew_chunk(0, 0)
            link.leave(1, 2)

            def gather_pass(k, r0, r1, ix, rank, carry, weight, extra=None, drain=0, end=None):
                with dve.Fori(r0, r1) as i:
                    for u in range(U + drain):
                        if u % HU == 0 and u < U:
                            half = slice(u, u + HU)
                            dve.wait_ge(s_done, k * ET + i * U + u + HU)
                            V.tensor_copy(ixr[:, half], ix[:, bass.ds(i * U + u, HU)])
                            V.tensor_copy(crr[:, half], carry[:, bass.ds(i * U + u, HU)]).then_inc(s_idx, 1)
                        if u < U:
                            of = rank[:, bass.ds(i * U + u, 1)]
                            if weight is None:
                                ins = V.tensor_scalar(M[:, u, :], irow[:], of, None, ALU.is_equal)
                            else:
                                ins = V.tensor_scalar(M[:, u, :], irow[:], of, weight[:, bass.ds(i * U + u, 1)],
                                                      ALU.is_equal, ALU.mult)
                            ins.then_inc(s_m, 1)
                        if extra:
                            extra(i, u)
                    if end:
                        end(i)

            def one_hots(t, lo, hi, ql, qh):
                V.tensor_scalar(lo_b[:, ql, :], irow_b[:], lo[:, bass.ds(t, 1)], None, ALU.is_equal)
                return V.tensor_scalar(hi_b[:, qh, :], irow_b[:, 0:NT], hi[:, bass.ds(t, 1)], None, ALU.is_equal)

            def count(i, u):
                t = i * U + u
                q = 2 * (u % 2)
                dve.wait_ge(s_cnt, t + 1)
                one_hots(t, s_lo, s_hi, q, q)
                one_hots(t, d_lo, d_hi, q + 1, q + 1).then_inc(s_oh, 1)

            def place(i, u):
                if u < U:
                    t = i * U + u
                    if u >= 4:
                        dve.wait_ge(s_pp, t - 3)
                    one_hots(t, s_lo, s_hi, u % 4, u % 8).then_inc(s_oh, 1)
                if 2 <= u < U + 2:
                    v = u - 2
                    t = i * U + v
                    dve.wait_ge(s_eq, 1 + t + 1)
                    V.tensor_tensor(eqm[:, v % 4, :], ps[:, 7, 0:P], before[:],
                                    ALU.mult).then_inc(s_eqm, 1)
                if 4 <= u < U + 4:
                    v = u - 4
                    t = i * U + v
                    dve.wait_ge(s_pp, t + 1)
                    dve.wait_ge(s_pos, 1 + t)
                    V.tensor_tensor_reduce(junk[:], hi_b[:, v % 8, :], ps[:, 5, 0:NT], 1.0, 0.0,
                                           ALU.mult, ALU.add, posr[:, v:v + 1]).then_inc(s_pos, 1)

            def place_end(i):
                dve.wait_ge(s_pos, 1 + i * U + U)
                V.tensor_copy(pos[:, bass.ds(i * U, U)], posr[:]).then_inc(s_posw, 1)

            def count_and_weigh(i):
                ew_chunk(i + 1, i)

            gather_pass(PASS_L0, 0, NR, ix_src, rank_d, carry_d, w_f, count, 0, count_and_weigh)
            link.leave(NR, 2)
            dve.wait_ge(s_ewc, EW_CHUNKS)
            V.memset(raw4[:, 3, NB - 1, :], 0.0).then_inc(s_sm, 1)

            dve.wait_ge(s_cnt, 2 + ET)
            V.tensor_copy(n_s[:], ps[:, 6, 0:NT])
            dve.wait_ge(s_pc, 4 + ET)
            for side, n in ((0, n_d), (1, n_s)):
                if side == 0:
                    ready(V.tensor_copy(n_d[:], ps[:, 7, 0:NT]))
                else:
                    signal(s_rdy)
                unit_done()
                link(V.tensor_copy(tot[:, side:side + 1], ps[0:NT, 4, 0:1]))
                ready(V.tensor_scalar(tot_b[:, side, :], ones[0:NT, :], tot[:, side:side + 1], None, ALU.mult))
                unit_done()
                e, lo_i, hi_i = small_i[:, 0, :], small_i[:, 1, :], small_i[:, 2, :]
                link(V.tensor_copy(base[:, side, :], ps[:, (5, 6)[side], 0:NT]))
                link(V.scalar_tensor_tensor(small[:, 0, :], base[:, side, :], -1.0, n[:], ALU.add, ALU.add))
                link(V.tensor_scalar(last_e[:, side, :], small[:, 0, :], 0.0, None, ALU.max))
                link(V.tensor_copy(e, last_e[:, side, :]))
                V.tensor_single_scalar(lo_i, e, P - 1, ALU.bitwise_and)
                link(V.tensor_single_scalar(hi_i, e, 7, ALU.logical_shift_right))
                V.tensor_copy(small[:, 1, :], lo_i)
                link(V.tensor_copy(small[:, 2, :], hi_i))
                V.scalar_tensor_tensor(end_ix[:, side, :], small[:, 1, :], float(ET), small[:, 2, :],
                                       ALU.mult, ALU.add).then_inc(s_eix, 1)
                link(V.tensor_scalar(last_e[:, side, :], small[:, 2, :], float(P), None, ALU.mult))

            def find_rows(side, n):
                dve.wait_ge(s_eg[side], 16 * NT)
                V.tensor_scalar(small[:, 0, :], n[:], 0.0, None, ALU.is_gt)
                link(V.scalar_tensor_tensor(small[:, 1, :], last_e[:, side, :], -float(ZROW), rank_end[:, side, :],
                                            ALU.add, ALU.add))
                link(V.tensor_tensor(small[:, 2, :], small[:, 1, :], small[:, 0, :], ALU.mult))
                V.tensor_scalar(fin[:, side, :], small[:, 2, :], float(ZROW), None, ALU.add).then_inc(s_tab, 1)

            V.tensor_scalar(small[:, 3, :], n_s[:], 1.0, None, ALU.max)
            link(V.tensor_scalar(eps1[:], eps_c[:], 1.0, None, ALU.add))
            link(V.reciprocal(inv_s[:], small[:, 3, :]))
            dve.wait_ge(s_meta[3], 96)
            signal(s_rdy)
            unit_done()
            link(from_pair(w_f[:], 1))
            find_rows(0, n_d)
            link.leave(1, link.k)

            def wait_group(ph, i):
                for j in range(GN):
                    dve.wait_ge(s_ag[j], 16 * (b("ag", ph) + i))

            def flat(t):
                return t[:, :, :].rearrange("p j d -> p (j d)")

            def xg(i):
                return group(X, i).rearrange("p j d -> p (j d)")

            def n0_x(i):
                first.turn(i, 2)
                wait_group(N0, i)
                ins = V.tensor_tensor(xg(i), xg(i), flat(AG), ALU.add)
                first(ins)
                V.sem_inc(s_a7, 1)
                first(V.scalar_tensor_tensor(xg(i), group(HN, i).rearrange("p j d -> p (j d)"), eps1[:], xg(i),
                                             ALU.mult, ALU.add))
                norm_step(N0, i)

            def rows_copy(ph):
                def step(i):
                    dve.wait_ge(s_a5, b("a5", ph) + i + 1)
                    dve.wait_ge(s_hst, 16 * (stores(ph) + i))
                    V.tensor_copy(flat(HS), bank(5)).then_inc(s_a6, 1)
                return step

            staged(dve, [(0, n0_x), (2, rows_copy(N0))])
            first.leave(NG, 2)
            norm.leave(NG, 2)

            def relation(i):
                at = big[:, bass.ds(i * D, D)]
                link.turn(i, B)
                for m in range(B):
                    c = comp_b[:, bass.ds(i * B + m, 1)]
                    if m == 0:
                        link(V.tensor_scalar(at, basis[:, m, :], c, None, ALU.mult))
                    else:
                        link(V.scalar_tensor_tensor(at, basis[:, m, :], c, at, ALU.mult, ALU.add))

            for l in range(LAYERS):
                args = (ix_src, rank_d, carry_d, w_f)
                if l == 0:
                    gather_pass(PASS_L1, 0, NR, *args, place, 4, place_end)
                elif l == 1:
                    gather_pass(PASS_L1 + l, 0, R, *args, end=relation)
                    link.leave(R, B)
                    gather_pass(PASS_L1 + l, R, NR, *args)
                else:
                    gather_pass(PASS_L1 + l, 0, NR, *args)
                ph = G0 + l

                def gru(i):
                    first.turn(i, 3)
                    dve.wait_ge(s_a3, b("a3", ph) + 3 * i + 2)
                    dve.wait_ge(s_a4, b("a4", ph) + 3 * i + 1)
                    first(V.scalar_tensor_tensor(tS[:], bank(3), b_hh[:, 2:3], rS[:], ALU.add, ALU.mult))
                    V.tensor_tensor(tS[:], tS[:], bank(2), ALU.add).then_inc(s_a8, 1)
                    dve.wait_ge(s_a4, b("a4", ph) + 3 * i + 3)
                    dve.wait_ge(s_a5, b("a5", ph) + i)
                    if l < LAYERS - 1:
                        dve.wait_ge(s_a10, b("a10", ph) + i)
                    first(V.tensor_tensor(dS, feat(i), nS[:], ALU.subtract))
                    first(V.tensor_tensor(dS, dS, zS[:], ALU.mult))
                    V.tensor_tensor(dS, dS, nS[:], ALU.add).then_inc(s_a8, 1)

                def gru_x(i):
                    dve.wait_ge(s_a5, b("a5", ph) + i + 1)
                    x_add(i)
                    norm_step(G2, i)

                def x_add(i):
                    last.turn(i, 1)
                    last(V.tensor_tensor(xg(i), xg(i), bank(5), ALU.add))
                    V.sem_inc(s_a7, 1)

                last = Chain(s_v2)
                if l < LAYERS - 1:
                    staged(dve, [(0, gru), (1, rows_copy(ph))])
                else:
                    staged(dve, [(0, gru), (1, gru_x)])
                    norm.leave(NG, 2)
                first.leave(NG, 3)

            dve.wait_ge(s_eg[2], 32)
            signal(s_rdy)
            unit_done()
            V.tensor_copy(erT[0:P, 0:2, :], ps[:, 4, 0:2 * R].rearrange("p (c r) -> p c r", r=R))
            ready(V.tensor_copy(erT[0:2 * DA, 2, :], ps[0:2 * DA, 4, 2 * R:3 * R]))
            unit_done()
            link(V.tensor_tensor(ahid[:, 0, :], ps[0:R, 5, 0:D], ab1[:], ALU.add))
            link(V.tensor_scalar(ahid[:, 0, :], ahid[:, 0, :], 0.0, None, ALU.max))
            V.tensor_tensor_reduce(ahid[:, 1, :], ahid[:, 0, :], aw2[:], 1.0, 0.0, ALU.mult, ALU.add,
                                   alog[:, 0:1]).then_inc(s_att, 1)
            dve.wait_ge(s_att, 2)
            ready(V.tensor_scalar(adiag[:], ident[0:R, 0:R], alog[:, 1:2], None, ALU.mult))
            unit_done()
            link(V.tensor_copy(alpha[:], ps[:, 4, 64:64 + R]))
            for r in range(R):
                ins = V.tensor_scalar(big[:, r * D:(r + 1) * D], big[:, r * D:(r + 1) * D], alpha[:, r:r + 1],
                                      None, ALU.mult)
            ready(ins)
            link.leave(1, link.k)

            with dve.Fori(0, NT // 2) as i:
                for q in range(2):
                    dve.wait_ge(s_tm, i * 2 + q + 1)
                    dve.wait_ge(s_ts[q], 16 * (1 + i))
                    V.tensor_copy(t_buf[q][:, 2 * BANK:4 * BANK], ps[:, 4 * q + 2:4 * q + 4, :]
                                  .rearrange("p b c -> p (b c)")).then_inc(s_te[1], 1)
            for q in range(2):
                dve.wait_ge(s_ts[q], 16 * (1 + NT // 2))
            gather_pass(PASS_L2, 0, PREP_AT, ix_t, rank_d, carry_d, None)
            dve.wait_ge(s_meta[0], 64)
            for k in range(2):
                ready(V.tensor_copy(flt[k], raw_pair[:, :, :, k]))
            unit_done()
            link(from_pair(src_f, 2))
            unit_done()
            link(from_pair(dst_f, 3))
            ready(V.tensor_copy(ix_q[:], dst_f))
            segments(src_f, carry_s[:], rank_s[:], 2, 3, s_sm)
            link.leave(1, link.k)
            gather_pass(PASS_L2, PREP_AT, NR, ix_t, rank_d, carry_d, None)
            find_rows(1, n_s)
            link.leave(1, link.k)

            def n2_x(i):
                first.turn(i, 2)
                wait_group(N2, i)
                dve.wait_ge(s_a3, b("a3", N2) + i + 1)
                for j in range(GN):
                    ins = V.scalar_tensor_tensor(tS[:, j * D:(j + 1) * D], ps[:, 0, j * D:(j + 1) * D],
                                                 n_d[:, bass.ds(i * GN + j, 1)], AG[:, j, :],
                                                 ALU.mult, ALU.add)
                first(ins)
                V.sem_inc(s_a7, 1)
                first(V.scalar_tensor_tensor(xg(i), tS[:], 0.0, xg(i), ALU.max, ALU.add))
                norm_step(N2, i)

            with dve.Fori(0, NG) as i:
                n2_x(i)
            first.leave(NG, 2)
            norm.leave(NG, 2)
            gather_pass(PASS_L3, 0, NR, ix_q, rank_s, carry_s, None)

            def n3_y(i):
                wait_group(N3, i)
                dve.wait_ge(s_a1, b("a1", N3) + i)
                for j in range(GN):
                    ins = V.scalar_tensor_tensor(HG[:, j, :], AG[:, j, :], inv_s[:, bass.ds(i * GN + j, 1)],
                                                 HN[:, bass.ds(i * GN + j, 1), :].rearrange("p t d -> p (t d)"),
                                                 ALU.mult, ALU.add)
                ins.then_inc(s_a8, 1)
                dve.wait_ge(s_a8, b("a8", N3) + i + 1)
                V.sem_inc(s_a7, 1)

            def n3_out(i):
                first.turn(i, 1)
                dve.wait_ge(s_a3, b("a3", N3) + i + 1)
                dve.wait_ge(s_hst, 16 * (stores(N3) + i))
                for j in range(GN):
                    ins = V.tensor_tensor(HS[:, j, :], ps[:, 0, j * D:(j + 1) * D], b3[:], ALU.add)
                first(ins)
                V.tensor_tensor(flat(HS), flat(HS), xg(i), ALU.add).then_inc(s_a6, 1)

            staged(dve, [(0, n3_y), (1, n3_out)])

        @block.scalar
        def _(act):
            A = nc.scalar

            def hold(s, value):
                act.wait_ge(s, value)
                act.sem_inc(s_hold[2], 1)

            act.sem_inc(s_pc, 4)
            for s in (s_hg, s_a2, s_a4, s_a10, s_lc, s_te[0]):
                act.sem_inc(s, 1)

            def normalise(ph, dst, free=None):
                def step(i):
                    hold(s_ln, b("ln", ph) + i + 1)
                    if free:
                        free(i)
                    for j in range(GN):
                        ins = A.activation(dst(i, j), X[:, bass.ds(i * GN + j, 1), :].rearrange("p t d -> p (t d)"),
                                           ACT.Relu, bias=nbias[:, bass.ds(i * GN + j, 1)],
                                           scale=rstd[:, bass.ds(i * GN + j, 1)])
                    ins.then_inc(s_hg, 1)
                return step

            def into_hn(i, j):
                return HN[:, bass.ds(i * GN + j, 1), :].rearrange("p t d -> p (t d)")

            def into_hg(i, j):
                return HG[:, j, :]

            with act.Fori(0, NG) as i:
                normalise(LN0, into_hn)(i)

            def gather_pass(k, r0, r1, extra=None, drain=0):
                with act.Fori(r0, r1) as i:
                    for u in range(U + drain):
                        if u < U:
                            if u % HU == 0:
                                act.wait_ge(s_ps[u // HU], 16 * (1 + k * NR + i))
                            act.wait_ge(s_done, U + k * ET + i * U + u + 1)
                            A.copy(PR[:, u, :], ps[:, u % 4, 0:D]).then_inc(s_pc, 1)
                        if extra:
                            extra(i, u)

            def place(i, u):
                if u < U:
                    t = i * U + u
                    act.wait_ge(s_loT, t + 1)
                    if u >= 4:
                        act.wait_ge(s_pp, t - 3)
                    A.copy(loT[:, u % 4, :], ps[:, 4, 0:P // 2].bitcast(BF16))
                    act.wait_ge(s_eq, 1 + t)
                    A.copy(run_s[:, u % 4, :], ps[:, 6, 0:NT]).then_inc(s_lc, 1)

            def copy_in(ph):
                def step(i):
                    act.wait_ge(s_a1, b("a1", ph) + i + 1)
                    if ph in (N0, N3):
                        if not (isinstance(i, int) and i == 0):
                            act.wait_ge(s_a3, b("a3", ph) + i)
                    elif not (isinstance(i, int) and i == 0):
                        act.wait_ge(s_a3, b("a3", ph) + 3 * i)
                    A.copy(aT[:], bank(4)).then_inc(s_a2, 1)
                return step

            gather_pass(PASS_L0, 0, NR)

            def hg_free(i):
                act.wait_ge(s_a1, b("a1", N0) + i)

            def n0_relu(i):
                act.wait_ge(s_a5, b("a5", N0) + i)
                hold(s_a3, b("a3", N0) + i + 1)
                A.activation(dS, bank(0), ACT.Relu, bias=b_node[:]).then_inc(s_a4, 1)
                A.activation(feat(i), bank(0), ACT.Relu, bias=b_node[:]).then_inc(s_a10, 1)

            staged(act, [(0, normalise(N0, into_hg, hg_free)), (0, copy_in(N0)), (1, n0_relu)])
            for l in range(LAYERS):
                gather_pass(PASS_L1 + l, 0, NR, place if l == 0 else None)
                ph = G0 + l

                def gates(i):
                    act.wait_ge(s_a3, b("a3", ph) + 3 * i + 1)
                    if not (isinstance(i, int) and i == 0):
                        act.wait_ge(s_a8, b("a8", ph) + 2 * i)
                    A.activation(rS[:], bank(0), ACT.Sigmoid, bias=b_rz[:, 0:1]).then_inc(s_a4, 1)
                    act.wait_ge(s_a3, b("a3", ph) + 3 * i + 3)
                    A.activation(zS[:], bank(1), ACT.Sigmoid, bias=b_rz[:, 1:2]).then_inc(s_a4, 1)
                    act.wait_ge(s_a8, b("a8", ph) + 2 * i + 1)
                    A.activation(nS[:], tS[:], ACT.Tanh, bias=b_ih[:, 2:3]).then_inc(s_a4, 1)

                def keep(i):
                    hold(s_a8, b("a8", ph) + 2 * i + 2)
                    A.copy(feat(i), dS).then_inc(s_a10, 1)

                stages = [(0, copy_in(ph))] + ([(1, keep)] if l < LAYERS - 1 else []) + [(0, gates)]
                if l == LAYERS - 1:
                    def hg_used(i):
                        if not (isinstance(i, int) and i == 0):
                            act.wait_ge(s_a9, b("a9", G2) + i)
                        act.wait_ge(s_hst, 16 * (stores(G2) + i))

                    def next_copy(i):
                        hold(s_a9, b("a9", G2) + i + 1)
                        A.copy(feat(i), bank(6)).then_inc(s_a10, 1)

                    stages += [(1, normalise(G2, into_hg, hg_used)), (2, next_copy)]
                staged(act, stages)
            act.wait_ge(s_att, 1)
            A.activation(alog[:, 1:2], alog[:, 0:1], ACT.Sigmoid, bias=ab2[:]).then_inc(s_att, 1)
            def table_h(i, q):
                A.copy(dS[:, q * P:(q + 1) * P], HT[:, bass.ds((2 * i + q) * P, P)]).then_inc(s_th, 1)

            for q in range(2):
                table_h(0, q)
            def table_out(i, last=False):
                for q in range(2):
                    hold(s_tm, i * 2 + q + 1)
                    if not last:
                        table_h(i + 1, q)
                    act.wait_ge(s_ts[q], 16 * (1 + i))
                    A.copy(t_buf[q][:, 0:2 * BANK], ps[:, 4 * q:4 * q + 2, :].rearrange("p b c -> p (b c)")) \
                        .then_inc(s_te[0], 1)

            with act.Fori(0, NT // 2 - 1) as i:
                table_out(i)
            table_out(NT // 2 - 1, last=True)
            gather_pass(PASS_L2, 0, NR)

            def update_in(i):
                hold(s_a3, b("a3", N2) + i)
                A.copy(aT[:], feat(i)).then_inc(s_a2, 1)

            staged(act, [(0, update_in), (1, normalise(N2, into_hn))])
            gather_pass(PASS_L3, 0, NR)
            staged(act, [(0, copy_in(N3))])


_INS = ["x", "src", "dst", "edge_attr_32", "edge_attr_32_n2", "edge_attr_64", "edge_attr_64_n2",
        "edge_type_16", "edge_weight", "L0_gnn_eps", "L1_gnn_W_node", "L1_gnn_b_node",
        "L1_gnn_conv_weight", "L1_gnn_w_ih", "L1_gnn_w_hh", "L1_gnn_b_ih", "L1_gnn_b_hh",
        "L2_gnn_weight", "L2_gnn_comp", "L2_gnn_attn_w1", "L2_gnn_attn_b1", "L2_gnn_attn_w2",
        "L2_gnn_attn_b2", "L2_gnn_update", "L3_gnn_W", "L3_gnn_b"]


def kernel(**inputs):
    import numpy as _np
    import concourse.bacc as _bacc
    from concourse import mybir as _mybir
    from concourse.bass_utils import run_bass_kernel_spmd as _run

    nc = _bacc.Bacc("TRN2", target_bir_lowering=False, num_devices=1)
    arrays, aps = {}, {}
    for name in _INS:
        v = _np.ascontiguousarray(inputs[name])
        arrays[f"in_{name}"] = v
        aps[name] = nc.dram_tensor(f"in_{name}", v.shape, _mybir.dt.from_np(v.dtype), kind="ExternalInput").ap()
    out = nc.dram_tensor("out_x", (N, D), F32, kind="ExternalOutput").ap()
    gnn_kernel(nc, aps, out)
    r = _run(nc, [arrays], core_ids=[0])
    return r.results[0]["out_x"]
```

```python
from contextlib import ExitStack, nullcontext

import concourse.bass as bass
from concourse import mybir

ALU = mybir.AluOpType
ACT = mybir.ActivationFunctionType
AX = mybir.AxisListType
F32 = mybir.dt.float32
BF16 = mybir.dt.bfloat16
I32 = mybir.dt.int32
U32 = mybir.dt.uint32

P = 128
D = 128
N = 6250
E = 100000
GN = 4
NG = -(-N // (P * GN))
NT = NG * GN
NP = NT * P
U = 16
HU = U // 2
ET = -(-E // (P * U)) * U
NR = ET // U
EP = ET * P
TB = 112
NB = ET // TB
ZROW = EP
PAD_KEY = NP - 1
R, B = 16, 8
LAYERS = 3
EW_P, EW_C = 125, 16
EW_N = E // EW_P
EW_CHUNKS = EW_N // EW_C
DE, DA = 64, 32
NN_FULL = N // P
N_REST = N - NN_FULL * P
BANK = 512
LN_EPS = 1e-5

PASS_L0, PASS_L1, PASS_L2, PASS_L3 = 0, 1, 1 + LAYERS, 2 + LAYERS
PLACE = (PASS_L1, PASS_L1 + 1)
VU = U // 2
SCT_LEFT = (2 * NR - 3 * NG) // 2
PREP_AT = 8


def gnn_kernel(nc, a, out):
    with ExitStack() as ctx:
        def sb(name, shape, dt=F32):
            return ctx.enter_context(nc.sbuf_tensor(name, shape, dt))

        def sem(name):
            return ctx.enter_context(nc.semaphore(name))

        def dram(name, shape, dt=F32):
            return nc.dram_tensor(name, shape, dt, kind="Internal").ap()

        h_rows = dram("h_rows", (NP, D))
        t_rows = dram("t_rows", (NP * R, D))
        seg_rows = dram("seg_rows", (EP + P, D))
        rank_flat = [dram(f"rank_flat_{side}", (P * ET, 1)) for side in ("dst", "src")]
        ew_flat = dram("ew_flat", (E,))
        by_src = dram("by_src", (EP, 2), U32)

        ps = ctx.enter_context(nc.psum_tensor("ps", [P, 8, BANK], F32))
        two = ps[:, :, :].rearrange("p (k b) c -> p k (b c)", b=2)

        irow = sb("irow", [P, P])
        irow_b = sb("irow_b", [P, P], BF16)
        icol = sb("icol", [P, 1])
        cols = sb("cols", [P, 6])
        ident = sb("ident", [P, P])
        ident_b = sb("ident_b", [P, P], BF16)
        before = sb("before", [P, P])
        upto = sb("upto", [P, P])
        shift = sb("shift", [P, P])
        last_to_0 = sb("last_to_0", [P, P])
        from_last = sb("from_last", [P, P])
        from_0 = sb("from_0", [P, P])
        ones = sb("ones", [P, P])
        zf = sb("zf", [P, P])
        zb = zf[:, 0:P // 2].bitcast(BF16)

        X = sb("X", [P, NT, D])
        HN = sb("HN", [P, NT, D])
        HT = sb("HT", [P, NP])
        AG = [sb("AG", [P, GN, D])]
        HG = sb("HG", [P, GN, D])
        HS = sb("HS", [P, GN, D])
        aT = sb("aT", [P, GN * P])
        rS = sb("rS", [P, GN * P])
        zS = sb("zS", [P, GN * P])
        nS = sb("nS", [P, GN * P])
        tS = sb("tS", [P, GN * P])
        bst = sb("bst", [P, GN, 6])
        mv = sb("mv", [P, GN, 2])
        var_e = sb("var_e", [P, NT])
        nmean = sb("nmean", [P, NT])
        rstd = sb("rstd", [P, NT])
        nbias = sb("nbias", [P, NT])
        mhalf = sb("mhalf", [P, GN])

        G = sb("G", [P, U, D])
        M = sb("M", [P, U, P])
        PR = sb("PR", [P, U, D])
        dS = PR[:, 0:GN, :].rearrange("p j d -> p (j d)")
        ixr = sb("ixr", [P, U], U32)
        crr = sb("crr", [P, U])
        nix = sb("nix", [P, 2, GN], U32)
        six = sb("six", [P, U], U32)
        spay = sb("spay", [P, U, 2], U32)

        raw = sb("raw", [P, 4 * NB * P])
        raw4 = raw[0:TB, :].rearrange("p (k b c) -> p k b c", k=4, c=P)
        raw4_i = raw[0:TB, :].bitcast(I32).rearrange("p (k b c) -> p k b c", k=4, c=P)
        raw_pair = raw[0:TB, 0:2 * NB * P].bitcast(U32).rearrange("p (b c k) -> p b c k", b=NB, k=2)
        za = raw[0:EW_P, 0:2 * EW_C * DE].rearrange("p (k c d) -> p k c d", k=2, d=DE)
        w_f = sb("w_f", [P, ET])
        s_lo = sb("s_lo", [P, ET])
        s_hi = sb("s_hi", [P, ET])
        d_lo = sb("d_lo", [P, ET])
        d_hi = sb("d_hi", [P, ET])
        rank_d = sb("rank_d", [P, ET])
        carry_d = sb("carry_d", [P, ET])
        rank_s, carry_s = s_lo, s_hi
        ix_src = sb("ix_src", [P, ET], U32)
        ix_dst = sb("ix_dst", [P, ET], U32)
        ix_t = sb("ix_t", [P, ET], U32)
        ix_q = ix_src
        pos = sb("pos", [P, ET], U32)
        hn = HN[:, :, :].rearrange("p t d -> p (t d)")
        tab = [hn[:, k * ET:(k + 1) * ET] for k in range(4)]
        src_f, dst_f, typ_f, tmp = tab
        tmp_i = hn[:, 4 * ET:5 * ET].bitcast(I32)
        flt0 = 5 * ET
        flt = [hn[0:TB, flt0 + k * NB * P:flt0 + (k + 1) * NB * P].rearrange("p (b c) -> p b c", c=P)
               for k in range(3)]
        n_d = sb("n_d", [P, NT])
        n_s = sb("n_s", [P, NT])
        base = sb("base", [P, 2, NT])
        fin = sb("fin", [P, 2, NT], U32)
        inv_s = sb("inv_s", [P, NT])
        small = nS[:, 0:4 * NT].rearrange("p (k t) -> p k t", t=NT)
        small_i = tS[:, 0:3 * NT].bitcast(I32).rearrange("p (k t) -> p k t", t=NT)
        last_e = sb("last_e", [P, 2, NT])
        end_ix = sb("end_ix", [P, 2, NT], U32)
        rank_end = sb("rank_end", [P, 2, NT])
        tot = sb("tot", [NT, 2])
        tot_b = sb("tot_b", [NT, 2, P])

        lo_b = sb("lo_b", [P, 4, P], BF16)
        hi_b = sb("hi_b", [P, 8, NT], BF16)
        loT = sb("loT", [P, 4, P])
        AG.append(loT)
        loT_b = loT[:, 0:2, :].rearrange("p k c -> p (k c)").bitcast(BF16).rearrange("p (k c) -> p k c", c=P)
        run_s = sb("run_s", [P, 4, NT])
        eqm = sb("eqm", [P, 4, P], BF16)
        hi_d = eqm[:, :, :].rearrange("p k c -> p (k c)")[:, 0:8 * NT].rearrange("p (k c) -> p k c", c=NT)
        junk = sb("junk", [P, NT])
        note = sb("note", [P, 16])
        posr = sb("posr", [P, VU])

        ew_t = HT[0:EW_P, 0:EW_N]
        t_buf = [x[:, :, :].rearrange("p u c -> p (u c)") for x in (M, G)]
        ew_r = sb("ew_r", [EW_P, EW_C])

        w_node = sb("w_node", [P, D])
        b_node = sb("b_node", [P, 1])
        eps_c = sb("eps_c", [P, 1])
        eps1 = sb("eps1", [P, 1])
        big = sb("big", [P, R * D])
        conv_raw = big[:, 0:LAYERS * D].rearrange("p (l d) -> p l d", l=LAYERS)
        ih_raw = big[:, 3 * D:6 * D].rearrange("p (l d) -> p l d", l=3)
        hh_raw = big[:, 6 * D:9 * D].rearrange("p (l d) -> p l d", l=3)
        l3_raw = big[:, 9 * D:10 * D]
        convT = big[:, 10 * D:13 * D].rearrange("p (l d) -> p l d", l=LAYERS)
        ihT = big[:, 13 * D:16 * D]
        hhT = sb("hhT", [P, 3 * D])
        wc = sb("wc", [P, LAYERS, 3 * D])
        b_ih = sb("b_ih", [P, 3])
        b_hh = sb("b_hh", [P, 3])
        b_rz = sb("b_rz", [P, 2])
        basis = sb("basis", [P, B, D])
        comp_b = sb("comp_b", [P, R * B])
        upd = sb("upd", [P, D])
        w3T = sb("w3T", [P, D])
        b3 = sb("b3", [P, D])
        erps = sb("erps", [R, 2 * D + 2 * DA])
        eix = sb("eix", [R, 2], I32)
        eix_u = sb("eix_u", [R, 2], U32)
        erT = sb("erT", [P, 3, R])
        aw1 = sb("aw1", [P, 3, D])
        ab1 = sb("ab1", [R, D])
        aw2 = sb("aw2", [R, D])
        ab2 = sb("ab2", [R, 1])
        ahid = tS[0:R, 0:2 * D].rearrange("p (k d) -> p k d", k=2)
        alog = sb("alog", [R, 2])
        adiag = sb("adiag", [R, R])
        alpha = sb("alpha", [P, R])

        s_iota = sem("s_iota")
        s_v = sem("s_v")
        s_v0 = sem("s_v0")
        s_v2 = sem("s_v2")
        s_v1 = sem("s_v1")
        s_pad = sem("s_pad")
        s_meta = [sem(f"s_meta{k}") for k in range(4)]
        s_x = sem("s_x")
        s_w = sem("s_w")
        s_rdy = sem("s_rdy")
        s_tr = sem("s_tr")
        s_dsm = sem("s_dsm")
        s_sm = sem("s_sm")
        s_eix = sem("s_eix")
        s_eg = [sem("s_eg0"), sem("s_eg1"), sem("s_eg2")]
        s_tab = sem("s_tab")
        s_ewl = sem("s_ewl")
        s_ewc = sem("s_ewc")
        s_att = sem("s_att")
        s_idx = sem("s_idx")
        s_px = sem("s_px")
        s_m = sem("s_m")
        s_g = [sem(f"s_g{u}") for u in range(U)]
        s_done = sem("s_done")
        s_pc = sem("s_pc")
        s_ps = [sem("s_ps0"), sem("s_ps1")]
        s_oh = sem("s_oh")
        s_cnt = sem("s_cnt")
        s_loT = sem("s_loT")
        s_lc = sem("s_lc")
        s_eq = sem("s_eq")
        s_eqm = sem("s_eqm")
        s_pp = sem("s_pp")
        s_pos = sem("s_pos")
        s_posw = sem("s_posw")
        s_sct = [sem("s_sct0"), sem("s_sct1")]
        s_scp = sem("s_scp")
        s_nx = sem("s_nx")
        s_hold = [sem(f"s_hold{k}") for k in range(3)]
        s_ag = [[sem(f"s_ag{slot}{j}") for j in range(GN)] for slot in range(2)]
        s_var = sem("s_var")
        s_rs = sem("s_rs")
        s_ln = sem("s_ln")
        s_hg = sem("s_hg")
        s_hst = sem("s_hst")
        s_a1 = sem("s_a1")
        s_a2 = sem("s_a2")
        s_a3 = sem("s_a3")
        s_a4 = sem("s_a4")
        s_a5 = sem("s_a5")
        s_a6 = sem("s_a6")
        s_a7 = sem("s_a7")
        s_a8 = sem("s_a8")
        s_a9 = sem("s_a9")
        s_a10 = sem("s_a10")
        s_te = [sem("s_te0"), sem("s_te1")]
        s_ts = [sem("s_ts0"), sem("s_ts1")]
        s_th = sem("s_th")
        s_tm = sem("s_tm")

        LN0, N0, G0, G1, G2, N2, N3 = range(7)
        per = {
            "ag": (0, 1, 1, 1, 1, 1, 1),
            "ln": (1, 1, 0, 0, 1, 1, 0),
            "a1": (0, 1, 1, 1, 1, 0, 1),
            "a3": (0, 1, 3, 3, 3, 1, 1),
            "a4": (0, 1, 3, 3, 3, 0, 0),
            "a5": (0, 1, 1, 1, 1, 0, 0),
            "a6": (0, 1, 1, 1, 0, 0, 1),
            "a7": (0, 1, 0, 0, 1, 1, 1),
            "a8": (0, 0, 2, 2, 2, 0, 1),
            "a2": (0, 1, 1, 1, 1, 1, 1),
            "a10": (0, 1, 1, 1, 1, 0, 0),
            "a9": (0, 0, 0, 0, 1, 0, 0),
            "hst": (1, 1, 1, 1, 1, 1, 1),
        }

        def b(name, phase):
            return 1 + NG * sum(per[name][:phase])

        def stores(phase):
            return b("hst", phase)

        def staged(eng, stages):
            deep = max(lag for lag, _ in stages)
            for s in range(deep):
                for lag, step in stages:
                    if s >= lag:
                        step(s - lag)
            with eng.Fori(deep, NG) as s:
                for lag, step in stages:
                    step(s - lag)
            for s in range(NG, NG + deep):
                for lag, step in stages:
                    if s - lag < NG:
                        step(s - lag)

        def staged_by_two(eng, stages):
            def run(stage, i, slot, nth):
                stage[1](*((i, slot, nth) if len(stage) == 3 else (i,)))

            deep = max(1, *(stage[0] for stage in stages))
            deep += (NG - deep) % 2
            for s in range(deep):
                for stage in stages:
                    i = s - stage[0]
                    if i >= 0:
                        run(stage, i, i % 2, i // 2)
            with eng.Fori(0, (NG - deep) // 2) as pair:
                for q in range(2):
                    for stage in stages:
                        i = deep + q - stage[0]
                        run(stage, pair * 2 + i, i % 2, pair + i // 2)
            for s in range(NG, NG + deep):
                for stage in stages:
                    i = s - stage[0]
                    if i < NG:
                        run(stage, i, i % 2, i // 2)

        def wait_group(eng, phase, slot, nth):
            before = sum(per["ag"][:phase]) * ((NG + 1 - slot) // 2)
            for j in range(GN):
                eng.wait_ge(s_ag[slot][j], 16 * (before + nth + 1))

        def rounds(eng, r0, r1):
            return nullcontext(r0) if r1 == r0 + 1 else eng.Fori(r0, r1)

        def first_round(i):
            return isinstance(i, int) and i % NR == 0

        def pass_with_places(gather_pass, k, place):
            def step(i, u):
                if u % 2 == 0:
                    place(i + PLACE.index(k) * NR, u // 2)

            gather_pass(k, 0, 1, extra=step)
            gather_pass(k, 1, NR, extra=step)

        def drain(k, place):
            for u in range(VU, VU + 4):
                place((PLACE.index(k) + 1) * NR - 1, u)

        def group(t, g):
            return t[:, bass.ds(g * GN, GN), :]

        def feat(g):
            return HT[:, bass.ds(g * GN * P, GN * P)]

        def bank(k, n=GN * P):
            return ps[:, k, 0:n]

        def quarters(k):
            return ps[:, k, :].rearrange("p (j d) -> p j d", j=GN)

        N_LOADS = 26
        block = ctx.enter_context(nc.Block())
        rows_of = h_rows.rearrange("(t p) d -> p t d", p=P)
        WHOLE = (E // P) // TB * TB * P
        ROWS = E // P - WHOLE // P
        REST = E - WHOLE - ROWS * P
        T0 = 4 * TB

        @block.sync
        def _(sp):
            def tile_load(dst, k, flat):
                sp.dma_start(dst[:, k, 0:NB - 1, :], flat[0:WHOLE].rearrange("(b p c) -> p b c", p=TB, c=P)) \
                    .then_inc(s_meta[k], 16)
                sp.dma_start(dst[0:ROWS, k, NB - 1, :], flat[WHOLE:E - REST].rearrange("(p c) -> p c", c=P)) \
                    .then_inc(s_meta[k], 16)
                sp.dma_start(dst[ROWS:ROWS + 1, k, NB - 1, 0:REST],
                             flat[E - REST:E].rearrange("(p c) -> p c", p=1)).then_inc(s_meta[k], 16)

            for s in (s_hst, *s_ps, *s_ts):
                sp.sem_inc(s, 16)
            sp.wait_ge(s_pad, 1)
            for k, name in enumerate(("src", "dst", "edge_type_16", "edge_weight")):
                tile_load(raw4_i if k < 3 else raw4, k, a[name])
            sp.dma_start(X[:, 0:NN_FULL, :], a["x"][0:NN_FULL * P].rearrange("(t p) d -> p t d", p=P)) \
                .then_inc(s_x, 16)
            sp.dma_start(X[0:N_REST, NN_FULL, :], a["x"][NN_FULL * P:N]).then_inc(s_x, 16)

            def load(dst, src):
                sp.dma_start(dst, src).then_inc(s_w, 16)

            def row(v, n):
                return v.rearrange("(a o) -> a o", a=1).broadcast_to((n, v.shape[0]))

            load(eps_c[:], row(a["L0_gnn_eps"], P))
            load(w_node[:], a["L1_gnn_W_node"])
            load(b_node[:], a["L1_gnn_b_node"].rearrange("(p c) -> p c", c=1))
            load(conv_raw, a["L1_gnn_conv_weight"].rearrange("l i o -> i l o"))
            load(ih_raw, a["L1_gnn_w_ih"].rearrange("(g o) i -> o g i", g=3))
            load(hh_raw, a["L1_gnn_w_hh"].rearrange("(g o) i -> o g i", g=3))
            for g in range(3):
                load(b_ih[:, g:g + 1], a["L1_gnn_b_ih"][g * D:(g + 1) * D].rearrange("(p c) -> p c", c=1))
                load(b_hh[:, g:g + 1], a["L1_gnn_b_hh"][g * D:(g + 1) * D].rearrange("(p c) -> p c", c=1))
            load(basis[:], a["L2_gnn_weight"].rearrange("b i o -> i b o"))
            load(comp_b[:, :], row(a["L2_gnn_comp"].rearrange("r b -> (r b)"), P))
            load(upd[:], a["L2_gnn_update"])
            load(l3_raw, a["L3_gnn_W"])
            load(b3[:], row(a["L3_gnn_b"], P))
            load(erps[:, 2 * D:2 * D + DA], a["edge_attr_32"][0:R])
            load(erps[:, 2 * D + DA:2 * D + 2 * DA], a["edge_attr_32_n2"][0:R])
            load(eix[:, 0:1], a["src"][0:R].rearrange("(p c) -> p c", c=1))
            load(eix[:, 1:2], a["dst"][0:R].rearrange("(p c) -> p c", c=1))
            load(aw1[:, 0:2, :], a["L2_gnn_attn_w1"][0:2 * D].rearrange("(c p) o -> p c o", p=P))
            load(aw1[0:2 * DA, 2, :], a["L2_gnn_attn_w1"][2 * D:2 * D + 2 * DA])
            load(ab1[:], row(a["L2_gnn_attn_b1"], R))
            load(aw2[:], row(a["L2_gnn_attn_w2"].rearrange("o a -> (o a)"), R))
            load(ab2[:], row(a["L2_gnn_attn_b2"], R))
            sp.dma_start(seg_rows[EP:EP + P], zf[:]).then_inc(s_dsm, 16)

            z_dram = a["edge_attr_64_n2"].rearrange("(p c) d -> p c d", p=EW_P)
            e_dram = a["edge_attr_64"].rearrange("(p c) d -> p c d", p=EW_P)

            def ew_load(c):
                sp.dma_start(za[:, 0, :, :], z_dram[:, bass.ds(c * EW_C, EW_C), :]).then_inc(s_ewl, 16)
                sp.dma_start(za[:, 1, :, :], e_dram[:, bass.ds(c * EW_C, EW_C), :]).then_inc(s_ewl, 16)

            with sp.Fori(0, NG) as i:
                sp.wait_ge(s_hg, b("ln", LN0) + i + 1)
                sp.dma_start(rows_of[:, bass.ds(i * GN, GN), :], group(HN, i)).then_inc(s_hst, 16)
            sp.wait_ge(s_sm, 1)
            sp.dma_start(rank_flat[0].rearrange("(p t) c -> p (t c)", p=P), rank_d[:]).then_inc(s_dsm, 16)
            ew_load(0)

            segs = seg_rows[0:EP].rearrange("(t p) d -> p t d", p=P)

            def seg_store(k, i, q):
                sp.wait_ge(s_pc, 4 + k * ET + i * U + (q + 1) * HU)
                sp.dma_start(segs[:, bass.ds(i * U + q * HU, HU), :], PR[:, q * HU:(q + 1) * HU, :]) \
                    .then_inc(s_ps[q], 16)

            def h_store(phase, src, ready, at):
                with sp.Fori(0, NG) as i:
                    sp.wait_ge(ready, i + at + 1)
                    sp.dma_start(rows_of[:, bass.ds(i * GN, GN), :], src(i)).then_inc(s_hst, 16)

            with sp.Fori(0, NR) as i:
                sp.wait_ge(s_ewc, i + 1)
                ew_load(i + 1)
                seg_store(PASS_L0, i, 0)
                seg_store(PASS_L0, i, 1)
            sp.wait_ge(s_sm, 2)
            sp.dma_start(ew_flat.rearrange("(p c) -> p c", p=EW_P), ew_t).then_inc(s_dsm, 16)
            sp.wait_ge(s_dsm, 48)
            tile_load(raw4, 3, ew_flat)
            h_store(N0, lambda i: HS[:], s_a6, b("a6", N0))
            for l in range(LAYERS):
                with sp.Fori(0, NR) as i:
                    seg_store(PASS_L1 + l, i, 0)
                    seg_store(PASS_L1 + l, i, 1)
                if l < LAYERS - 1:
                    h_store(G0 + l, lambda i: HS[:], s_a6, b("a6", G0 + l))
                else:
                    h_store(G0 + l, lambda i: HG[:], s_hg, b("ln", G0 + l))
            t_out = t_rows.rearrange("(t p r) d -> p t (r d)", p=P, r=R)
            with sp.Fori(0, NT // 2) as i:
                for q in range(2):
                    for h in range(2):
                        sp.wait_ge(s_te[h], 1 + i * 2 + q + 1)
                    sp.dma_start(t_out[:, bass.ds(2 * i + q, 1), :].rearrange("p t c -> p (t c)"), t_buf[q]) \
                        .then_inc(s_ts[q], 16)
            for q in range(2):
                sp.wait_ge(s_sct[q], 16 * HU * ((2 - q) * NG + SCT_LEFT + q))
            sp.dma_start(raw_pair.rearrange("p b c k -> p b (c k)"),
                         by_src.rearrange("(b p c) k -> p b (c k)", p=TB, c=P)).then_inc(s_meta[0], 16)
            with sp.Fori(0, PREP_AT) as i:
                seg_store(PASS_L2, i, 0)
                seg_store(PASS_L2, i, 1)
            sp.wait_ge(s_sm, 3)
            sp.dma_start(rank_flat[1].rearrange("(p t) c -> p (t c)", p=P), rank_s[:]).then_inc(s_dsm, 16)
            with sp.Fori(PREP_AT, NR) as i:
                seg_store(PASS_L2, i, 0)
                seg_store(PASS_L2, i, 1)
            h_store(N2, lambda i: group(HN, i), s_hg, b("ln", N2))
            with sp.Fori(0, NR) as i:
                seg_store(PASS_L3, i, 0)
                seg_store(PASS_L3, i, 1)
            out_of = out[0:NN_FULL * P].rearrange("(t p) d -> p t d", p=P)
            with sp.Fori(0, NG - 1) as i:
                sp.wait_ge(s_a6, b("a6", N3) + i + 1)
                sp.dma_start(out_of[:, bass.ds(i * GN, GN), :], HS[:]).then_inc(s_hst, 16)
            sp.wait_ge(s_a6, b("a6", N3) + NG)
            sp.dma_start(out[NN_FULL * P:N], HS[0:N_REST, NN_FULL - (NG - 1) * GN, :]).then_inc(s_hst, 16)
            sp.wait_ge(s_hst, 16 * (stores(N3) + NG))

        @block.gpsimd
        def _(pool):
            def hold(s, value):
                pool.wait_ge(s, value)
                pool.sem_inc(s_hold[0], 1)

            for s in (s_rs, s_ln, s_nx):
                pool.sem_inc(s, 1)
            nc.gpsimd.iota(irow[:], [[1, P]], base=0, channel_multiplier=0,
                           allow_small_or_imprecise_dtypes=True)
            nc.gpsimd.iota(icol[:], [[0, 1]], base=0, channel_multiplier=1,
                           allow_small_or_imprecise_dtypes=True).then_inc(s_iota, 1)

            def gather_pass(k, r0, r1, table):
                with pool.Fori(r0, r1) as i:
                    for q in range(2):
                        if k < PASS_L2:
                            hold(s_done, k * ET + i * U + (q + 1) * HU)
                            nc.gpsimd.tensor_copy(ixr[:, q * HU:(q + 1) * HU],
                                                  ix_src[:, bass.ds(i * U + q * HU, HU)]).then_inc(s_px, 1)
                            hold(s_px, 2 * (k * NR + i) + q + 1)
                        else:
                            hold(s_idx, 2 * (k * NR + i) + q + 1)
                        for u in range(q * HU, (q + 1) * HU):
                            nc.gpsimd.indirect_dma_start(
                                G[:, u, :], None, table,
                                bass.IndirectOffsetOnAxis(ap=ixr[:, u:u + 1], axis=0)).then_inc(s_g[u], 16)

            def deviation(phase):
                def step(i):
                    at = bass.ds(i * GN, GN)
                    hold(s_var, b("ln", phase) + i + 1)
                    nc.gpsimd.tensor_tensor(rstd[:, at], var_e[:, at], mhalf[:], ALU.pow).then_inc(s_rs, 1)
                    hold(s_rs, b("ln", phase) + i + 1)
                    nc.gpsimd.tensor_tensor(nbias[:, at], nmean[:, at], rstd[:, at], ALU.mult).then_inc(s_ln, 1)
                return step

            def node_gather(phase, k, side, used, at, beside=None):
                pool.wait_ge(s_ps[0], 16 * (1 + NR * (k + 1)))
                pool.wait_ge(s_ps[1], 16 * (1 + NR * (k + 1)))
                pool.wait_ge(s_dsm, 32)
                pool.wait_ge(s_tab, side + 1)

                def gather(i, slot, nth):
                    if not (isinstance(i, int) and i == 0):
                        hold(used, at + i - 1)
                    nc.gpsimd.tensor_copy(nix[:, slot, :], fin[:, side, bass.ds(i * GN, GN)]).then_inc(s_nx, 1)
                    hold(s_nx, b("ag", phase) + i + 1)
                    for j in range(GN):
                        nc.gpsimd.indirect_dma_start(
                            AG[slot][:, j, :], None, seg_rows,
                            bass.IndirectOffsetOnAxis(ap=nix[:, slot, j:j + 1], axis=0)) \
                            .then_inc(s_ag[slot][j], 16)

                staged_by_two(pool, [(0, gather, True)] + ([(0, beside)] if beside else []) +
                       ([(1, deviation(phase))] if per["ln"][phase] else []))

            def rank_gather(side):
                pool.wait_ge(s_eix, side + 1)
                pool.wait_ge(s_dsm, (32, 64)[side])
                for t in range(NT):
                    nc.gpsimd.indirect_dma_start(
                        rank_end[:, side, t:t + 1], None, rank_flat[side],
                        bass.IndirectOffsetOnAxis(ap=end_ix[:, side, t:t + 1], axis=0)) \
                        .then_inc(s_eg[side], 16)

            def scatter_half(h, q, before):
                lo = q * HU
                if not (isinstance(before, int) and before == 0):
                    hold(s_sct[q], 16 * HU * before)
                at = bass.ds(h * HU, HU)
                nc.gpsimd.tensor_copy(six[:, lo:lo + HU], pos[:, at])
                nc.gpsimd.tensor_copy(spay[:, lo:lo + HU, 0], ix_src[:, at])
                nc.gpsimd.tensor_copy(spay[:, lo:lo + HU, 1], ix_dst[:, at]).then_inc(s_scp, 1)
                hold(s_scp, h + 1)
                for u in range(lo, lo + HU):
                    nc.gpsimd.indirect_dma_start(
                        by_src, bass.IndirectOffsetOnAxis(ap=six[:, u:u + 1], axis=0),
                        spay[:, u, :], None).then_inc(s_sct[q], 16)

            with pool.Fori(0, NG) as i:
                deviation(LN0)(i)
            pool.wait_ge(s_hst, 16 * stores(N0))
            pool.wait_ge(s_sm, 1)
            gather_pass(PASS_L0, 0, NR, h_rows)
            rank_gather(0)
            node_gather(N0, PASS_L0, 0, s_a7, b("a7", N0))
            for l in range(LAYERS):
                pool.wait_ge(s_hst, 16 * stores(G0 + l))
                gather_pass(PASS_L1 + l, 0, NR, h_rows)
                beside = None
                if l < len(PLACE):
                    pool.wait_ge(s_posw, NR * (l + 1))
                if l >= len(PLACE) - 1:
                    q = l - (len(PLACE) - 1)

                    def beside(i, q=q):
                        if q == 0:
                            scatter_half(i, 0, i)
                        else:
                            scatter_half(NG + 2 * i, 0, NG + i)
                            scatter_half(NG + 2 * i + 1, 1, i)
                node_gather(G0 + l, PASS_L1 + l, 0, s_a1, b("a1", G0 + l), beside)
                if l == LAYERS - 1:
                    pool.wait_ge(s_hst, 16 * b("hst", N2))
                    pool.wait_ge(s_eix, 2)
                    for c in range(2):
                        nc.gpsimd.indirect_dma_start(
                            erps[:, c * D:(c + 1) * D], None, h_rows,
                            bass.IndirectOffsetOnAxis(ap=eix_u[:, c:c + 1], axis=0)).then_inc(s_eg[2], 16)
            with pool.Fori(0, SCT_LEFT) as i:
                for q in range(2):
                    scatter_half(3 * NG + 2 * i + q, q, (2 - q) * NG + i)
            scatter_half(2 * NR - 1, 1, NG + SCT_LEFT)
            for q in range(2):
                pool.wait_ge(s_ts[q], 16 * (1 + NT // 2))
            gather_pass(PASS_L2, 0, PREP_AT + 1, t_rows)
            rank_gather(1)
            gather_pass(PASS_L2, PREP_AT + 1, NR, t_rows)
            node_gather(N2, PASS_L2, 0, s_a7, b("a7", N2))
            pool.wait_ge(s_hst, 16 * stores(N3))
            gather_pass(PASS_L3, 0, NR, h_rows)
            node_gather(N3, PASS_L3, 1, s_a7, b("a7", N3))

        @block.tensor
        def _(pe):
            units = [0]

            def unit():
                units[0] += 1
                pe.wait_ge(s_rdy, units[0])

            def mm(dst, lhsT, rhs, start=True, stop=True):
                return nc.tensor.matmul(dst, lhsT, rhs, start=start, stop=stop, skip_group_check=True)

            def by_edge(k, tiles):
                unit()
                for c in range(NB):
                    at = c * TB if c < 4 else BANK + (c - 4) * TB
                    last = nc.tensor.transpose(two[:, k, at:at + TB], tiles[:, c, :], ident[0:TB, 0:TB])
                last.then_inc(s_tr, 1)

            def over(k, lhsT, rhs):
                mm(two[:, k, 0:BANK], lhsT, rhs[:, 0:BANK])
                return mm(two[:, k, BANK:ET], lhsT, rhs[:, BANK:ET])

            def previous_keys(k, keys):
                unit()
                mm(two[:, k, 0:BANK], shift[:], keys[:, 0:BANK], stop=False)
                mm(two[:, k, 1:BANK], last_to_0[:], keys[:, 0:BANK - 1], start=False)
                mm(two[:, k, BANK:ET], shift[:], keys[:, BANK:ET], stop=False)
                mm(two[:, k, BANK:ET], last_to_0[:], keys[:, BANK - 1:ET - 1], start=False).then_inc(s_tr, 1)

            def segment_units(k0, k1, keys, fresh, same, rank):
                previous_keys(k0, keys)
                unit()
                over(k1, upto[:], fresh).then_inc(s_tr, 1)
                unit()
                over(k0, from_0[:], same)
                over(k1, from_last[:], rank).then_inc(s_tr, 1)

            pe.sem_inc(s_done, U)
            pe.sem_inc(s_cnt, 4)
            for s in (s_a1, s_a3, s_a5, s_a9, s_eq):
                pe.sem_inc(s, 1)
            for k in range(3):
                by_edge(k, flt[k])
            by_edge(3, raw4[:, 3])
            segment_units(2, 3, dst_f, tab[3], carry_d, rank_d)
            unit()
            for l in range(LAYERS):
                nc.tensor.transpose(ps[:, 0, l * D:(l + 1) * D], conv_raw[:, l, :], ident[:])
                nc.tensor.transpose(ps[:, 1, l * D:(l + 1) * D], ih_raw[:, l, :], ident[:])
                nc.tensor.transpose(ps[:, 2, l * D:(l + 1) * D], hh_raw[:, l, :], ident[:])
            nc.tensor.transpose(ps[:, 3, 0:D], l3_raw, ident[:]).then_inc(s_tr, 1)
            unit()
            for l in range(LAYERS):
                last = mm(ps[:, 4 + l, 0:3 * D], convT[:, l, :], ihT)
            last.then_inc(s_tr, 1)
            unit()
            mm(ps[:, 6, 0:NT], zb, zb[:, 0:NT])
            mm(ps[:, 7, 0:NT], zb, zb[:, 0:NT]).then_inc(s_tr, 1)

            def gather_pass(k, r0, r1, extra=None):
                with rounds(pe, r0, r1) as i:
                    for u in range(U):
                        t = i * U + u
                        pe.wait_ge(s_m, k * ET + t + 1)
                        pe.wait_ge(s_g[u], 16 * (k * NR + i + 1))
                        mm(ps[:, u % 4, 0:D], M[:, u, :], G[:, u, :], stop=False)
                        pe.wait_ge(s_pc, k * ET + t + 4)
                        mm(ps[0:1, u % 4, 0:D], crr[:, u:u + 1], PR[:, (u - 1) % U, :],
                           start=False).then_inc(s_done, 1)
                        if extra:
                            extra(i, u)

            def count(i, u):
                pe.wait_ge(s_oh, i * U + u + 1)
                mm(ps[:, 6, 0:NT], lo_b[:, u % 4, :], hi_b[:, u % 8, :], start=False)
                mm(ps[:, 7, 0:NT], loT_b[:, u % 4, :], hi_d[:, u % 8, :], start=False).then_inc(s_cnt, 1)

            def place(i, u):
                t = i * VU + u
                back = u if first_round(i) else VU
                if u < VU:
                    pe.wait_ge(s_oh, ET + t + 1)
                    pe.wait_ge(s_lc, 1 + t)
                    nc.tensor.transpose(ps[:, 4, 0:P // 2].bitcast(BF16), lo_b[:, u % 4, :], ident_b[:]) \
                        .then_inc(s_loT, 1)
                if back >= 1 and u < VU + 1:
                    v = (u - 1) % VU
                    pe.wait_ge(s_lc, 1 + t)
                    if back >= 2:
                        pe.wait_ge(s_eqm, t - 1)
                    mm(ps[:, 7, 0:P], loT[:, v % 4, :], loT[:, v % 4, :])
                    mm(ps[:, 6, 0:NT], lo_b[:, v % 4, :], hi_b[:, v, :], start=False).then_inc(s_eq, 1)
                if back >= 3 and u < VU + 3:
                    v = (u - 3) % VU
                    pe.wait_ge(s_eqm, t - 2)
                    if back >= 4:
                        pe.wait_ge(s_pos, 1 + t - 3)
                    mm(ps[:, 5, 0:NT], loT[:, v % 4, :], run_s[:, v % 4, :], stop=False)
                    mm(ps[:, 5, 0:NT], eqm[:, v % 4, :], hi_b[:, v, :], start=False).then_inc(s_pp, 1)

            def totals(side, counts, to):
                unit()
                mm(ps[0:NT, 4, 0:1], counts[:], ones[:, 0:1]).then_inc(s_tr, 1)
                unit()
                mm(ps[:, to, 0:NT], before[:], counts[:], stop=False)
                mm(ps[:, to, 0:NT], tot_b[:, side, :], before[0:NT, 0:NT], start=False).then_inc(s_tr, 1)

            def turn(dst, src, done, rows=False):
                for j in range(GN):
                    last = nc.tensor.transpose(ps[:, dst, j * P:(j + 1) * P], src(j), ident[:])
                last.then_inc(done, 1)

            def new_h(j):
                return dS[:, j * P:(j + 1) * P]

            gather_pass(PASS_L0, 0, NR, count)
            totals(0, n_d, 5)
            by_edge(1, raw4[:, 3])

            def n0_in(i):
                pe.wait_ge(s_hg, b("ln", N0) + i + 1)
                pe.wait_ge(s_a2, b("a2", N0) + i)
                turn(4, lambda j: HG[:, j, :], s_a1)

            def n0_mm(i):
                pe.wait_ge(s_a2, b("a2", N0) + i + 1)
                pe.wait_ge(s_a10, b("a10", N0) + i)
                mm(bank(0), w_node[:], aT[:]).then_inc(s_a3, 1)

            def n0_back(i):
                pe.wait_ge(s_a4, b("a4", N0) + i + 1)
                pe.wait_ge(s_a6, b("a6", N0) + i)
                turn(5, new_h, s_a5)

            staged(pe, [(0, n0_in), (1, n0_mm), (2, n0_back)])
            totals(1, n_s, 6)

            for l in range(LAYERS):
                pe.wait_ge(s_a10, b("a10", G0 + l))
                k = PASS_L1 + l
                if k in PLACE:
                    pass_with_places(gather_pass, k, place)
                    drain(k, place)
                else:
                    gather_pass(k, 0, NR)
                ph = G0 + l

                def gru_gates(i, slot, nth):
                    wait_group(pe, ph, slot, nth)
                    pe.wait_ge(s_a2, b("a2", ph) + i)
                    turn(4, lambda j: AG[slot][:, j, :], s_a1)
                    pe.wait_ge(s_a4, b("a4", ph) + 3 * i - 2)
                    if not (isinstance(i, int) and i == 0):
                        pe.wait_ge(s_a8, b("a8", ph) + 2 * i - 1)
                    mm(bank(0), hhT[:, 0:D], feat(i), stop=False)
                    mm(bank(3), hhT[:, 2 * D:3 * D], feat(i))
                    pe.wait_ge(s_a2, b("a2", ph) + i + 1)
                    mm(bank(0), wc[:, l, 0:D], aT[:], start=False).then_inc(s_a3, 1)
                    mm(bank(2), wc[:, l, 2 * D:3 * D], aT[:]).then_inc(s_a3, 1)
                    pe.wait_ge(s_a4, b("a4", ph) + 3 * i - 1)
                    mm(bank(1), hhT[:, D:2 * D], feat(i), stop=False)
                    mm(bank(1), wc[:, l, D:2 * D], aT[:], start=False).then_inc(s_a3, 1)

                def gru_back(i):
                    pe.wait_ge(s_a8, b("a8", ph) + 2 * i + 2)
                    if l < LAYERS - 1:
                        pe.wait_ge(s_a6, b("a6", ph) + i)
                    else:
                        pe.wait_ge(s_a7, b("a7", G2) + i)
                    turn(5, new_h, s_a5)

                def next_in(i):
                    pe.wait_ge(s_hg, b("ln", G2) + i + 1)
                    pe.wait_ge(s_a10, b("a10", G2) + i)
                    turn(6, lambda j: HG[:, j, :], s_a9)

                staged_by_two(pe, [(0, gru_gates, True), (1, gru_back)] + ([(2, next_in)] if l == LAYERS - 1 else []))

            unit()
            for c, w in ((0, D), (1, D), (2, 2 * DA)):
                last = nc.tensor.transpose(ps[0:w, 4, c * R:(c + 1) * R], erps[:, c * D:c * D + w],
                                           ident[0:R, 0:R])
            last.then_inc(s_tr, 1)
            unit()
            for c, w in ((0, D), (1, D), (2, 2 * DA)):
                last = mm(ps[0:R, 5, 0:D], erT[0:w, c, :], aw1[0:w, c, :], start=c == 0, stop=c == 2)
            last.then_inc(s_tr, 1)
            unit()
            mm(ps[:, 4, 64:64 + R], ones[0:R, :], adiag[:]).then_inc(s_tr, 1)
            unit()
            with pe.Fori(0, NT // 2) as i:
                for q in range(2):
                    for h in range(2):
                        pe.wait_ge(s_te[h], 1 + i * 2 + q)
                    pe.wait_ge(s_th, i * 2 + q + 1)
                    for c in range(4):
                        last = mm(bank(4 * q + c), dS[:, q * P:(q + 1) * P],
                                  big[:, c * BANK:(c + 1) * BANK])
                    last.then_inc(s_tm, 1)
            for h in range(2):
                pe.wait_ge(s_te[h], 1 + NT)
            gather_pass(PASS_L2, 0, PREP_AT)
            by_edge(2, flt[0])
            by_edge(3, flt[1])
            segment_units(2, 3, src_f, tab[3], carry_s, rank_s)
            gather_pass(PASS_L2, PREP_AT, NR)

            def n2_mm(i):
                pe.wait_ge(s_a7, b("a7", N2) + i)
                pe.wait_ge(s_a2, b("a2", N2) + i + 1)
                for j in range(GN):
                    last = mm(ps[:, 0, j * D:(j + 1) * D], aT[:, j * P:(j + 1) * P], upd[:])
                last.then_inc(s_a3, 1)

            staged(pe, [(0, n2_mm)])
            gather_pass(PASS_L3, 0, NR)

            def n3_in(i):
                pe.wait_ge(s_a8, b("a8", N3) + i + 1)
                pe.wait_ge(s_a2, b("a2", N3) + i)
                turn(4, lambda j: HG[:, j, :], s_a1)

            def n3_mm(i):
                pe.wait_ge(s_a2, b("a2", N3) + i + 1)
                pe.wait_ge(s_a6, b("a6", N3) + i)
                for j in range(GN):
                    last = mm(ps[:, 0, j * D:(j + 1) * D], aT[:, j * P:(j + 1) * P], w3T[:])
                last.then_inc(s_a3, 1)

            staged(pe, [(0, n3_in), (1, n3_mm)])

        @block.vector
        def _(dve):
            V = nc.vector

            class Chain:

                def __init__(self, s):
                    self.s, self.base, self.k, self.at = s, 0, 0, 0

                def __call__(self, ins):
                    self.k += 1
                    ins.then_inc(self.s, 1)
                    dve.wait_ge(self.s, self.at + self.base + self.k)

                def turn(self, i, steps):
                    self.k, self.at = 0, i * steps

                def leave(self, turns, steps):
                    assert self.k == steps
                    self.base, self.k, self.at = self.base + turns * steps, 0, 0

            link, first, norm = Chain(s_v), Chain(s_v0), Chain(s_v1)

            def hold(s, value):
                dve.wait_ge(s, value)
                dve.sem_inc(s_hold[1], 1)

            noted = [0]

            def signal(s):
                V.memset(note[:, noted[0]:noted[0] + 1], 0.0).then_inc(s, 1)
                noted[0] += 1

            units = [0]

            def ready(ins):
                ins.then_inc(s_rdy, 1)

            def unit_done():
                units[0] += 1
                dve.wait_ge(s_tr, units[0])

            for s in (s_var, s_a6, s_a7, s_a8, s_pos, s_te[1]):
                dve.sem_inc(s, 1)
            V.memset(raw4_i[:, 0:2, NB - 1, :], PAD_KEY)
            V.memset(raw4_i[:, 2, NB - 1, :], 0)
            V.memset(raw4[:, 3, NB - 1, :], 0.0)
            V.memset(zf[:], 0.0)
            V.memset(ones[:], 1.0)
            V.memset(mhalf[:], -0.5)
            V.memset(PR[:], 0.0)
            V.memset(X[:, NN_FULL:NT, :], 0.0).then_inc(s_pad, 1)

            dve.wait_ge(s_iota, 1)
            link(V.tensor_scalar(cols[:, 0:1], icol[:], 0.0, None, ALU.is_gt))
            V.tensor_scalar(cols[:, 1:2], icol[:], 1.0, None, ALU.add)
            V.tensor_scalar(cols[:, 2:3], icol[:], float(P - 1), None, ALU.is_equal)
            link(V.tensor_scalar(cols[:, 3:4], icol[:], 0.0, None, ALU.is_equal))
            V.tensor_copy(irow_b[:], irow[:])
            V.tensor_scalar(ident[:], irow[:], icol[:], None, ALU.is_equal)
            V.tensor_scalar(ident_b[:], irow[:], icol[:], None, ALU.is_equal)
            V.tensor_scalar(before[:], irow[:], icol[:], None, ALU.is_gt)
            V.tensor_scalar(upto[:], irow[:], icol[:], cols[:, 0:1], ALU.is_ge, ALU.mult)
            V.tensor_scalar(shift[:], irow[:], cols[:, 1:2], None, ALU.is_equal)
            V.tensor_scalar(last_to_0[:], irow[:], 0.0, cols[:, 2:3], ALU.is_equal, ALU.mult)
            V.tensor_scalar(from_last[:], ones[:], cols[:, 2:3], None, ALU.mult)
            link(V.tensor_scalar(from_0[:], ones[:], cols[:, 3:4], None, ALU.mult))

            for k in range(3):
                dve.wait_ge(s_meta[k], 48)
                ready(V.tensor_copy(flt[k], raw4_i[:, k]))
            dve.wait_ge(s_meta[3], 48)
            signal(s_rdy)

            def from_pair(dst, k):
                V.tensor_copy(dst[:, 0:T0], two[:, k, 0:T0])
                return V.tensor_copy(dst[:, T0:ET], two[:, k, BANK:BANK + ET - T0])

            for k, dst in enumerate((src_f, dst_f, typ_f, w_f[:])):
                unit_done()
                link(from_pair(dst, k))
            V.tensor_copy(ix_src[:], src_f)
            V.tensor_copy(ix_dst[:], dst_f)
            V.scalar_tensor_tensor(ix_t[:], src_f, float(R), typ_f, ALU.mult, ALU.add)
            shifted = tmp.bitcast(I32)
            for key, lo, hi in ((src_f, s_lo, s_hi), (dst_f, d_lo, d_hi)):
                link(V.tensor_copy(tmp_i, key))
                link(V.tensor_single_scalar(shifted, tmp_i, 7, ALU.logical_shift_right))
                link(V.tensor_copy(hi[:], shifted))
                link(V.scalar_tensor_tensor(lo[:], hi[:], -float(P), key, ALU.mult, ALU.add))
            def segments(keys, same, rank, k0, k1, sm):
                fresh = tab[3]
                unit_done()
                V.tensor_tensor(same[:, 0:BANK], two[:, k0, 0:BANK], keys[:, 0:BANK], ALU.is_equal)
                link(V.tensor_tensor(same[:, BANK:ET], two[:, k0, BANK:ET], keys[:, BANK:ET], ALU.is_equal))
                link(V.memset(same[0:1, 0:1], 0.0))
                ready(V.tensor_scalar(fresh, same, -1.0, 1.0, ALU.mult, ALU.add))
                unit_done()
                ready(V.tensor_copy(rank, two[:, k1, 0:ET]))
                unit_done()
                link(V.tensor_copy(fresh, two[:, k0, 0:ET]))
                link(V.memset(same[:, 0:1], 0.0))
                link(V.scalar_tensor_tensor(same[:, 1:ET], two[:, k1, 0:ET - 1], icol[:], fresh[:, 1:ET],
                                            ALU.is_equal, ALU.mult))
                signal(s_sm)

            signal(s_rdy)
            segments(dst_f, carry_d[:], rank_d[:], 2, 3, s_sm)
            def norm_step(ph, i):
                norm.turn(i, 2)
                dve.sem_inc(s_hold[1], 1)
                for j in range(GN):
                    last = V.bn_stats(bst[:, j, :], X[:, bass.ds(i * GN + j, 1), :].rearrange("p t d -> p (t d)"))
                norm(last)
                dve.sem_inc(s_hold[1], 1)
                for j in range(GN):
                    last = V.bn_aggr(mv[:, j, :], bst[:, j, :])
                norm(last)
                V.tensor_scalar(var_e[:, bass.ds(i * GN, GN)], mv[:, :, 1], LN_EPS, None, ALU.add)
                V.tensor_scalar(nmean[:, bass.ds(i * GN, GN)], mv[:, :, 0], -1.0, None, ALU.mult) \
                    .then_inc(s_var, 1)

            dve.wait_ge(s_x, 32)
            with dve.Fori(0, NG) as i:
                norm_step(LN0, i)
            norm.leave(NG, 2)

            dve.wait_ge(s_w, 16 * N_LOADS)
            signal(s_rdy)
            unit_done()
            V.tensor_copy(convT, ps[:, 0, 0:3 * D].rearrange("p (l d) -> p l d", l=LAYERS))
            V.tensor_copy(ihT, ps[:, 1, 0:3 * D])
            V.tensor_copy(hhT[:], ps[:, 2, 0:3 * D])
            ready(V.tensor_copy(w3T[:], ps[:, 3, 0:D]))
            unit_done()
            link(V.tensor_copy(wc[:], ps[:, 4:4 + LAYERS, 0:3 * D]))
            V.tensor_tensor(b_rz[:], b_ih[:, 0:2], b_hh[:, 0:2], ALU.add)
            V.tensor_copy(eix_u[:], eix[:])
            V.memset(ahid, 0.0)
            signal(s_rdy)
            unit_done()

            def ew_chunk(c, turn):
                link.turn(turn, 2)
                dve.wait_ge(s_ewl, 32 * (c + 1))
                link(V.tensor_tensor(za[:, 0, :, :], za[:, 0, :, :], za[:, 1, :, :], ALU.mult))
                link(V.tensor_reduce(ew_r[:], za[:, 0, :, :], AX.X, ALU.add))
                V.tensor_copy(ew_t[:, bass.ds(c * EW_C, EW_C)], ew_r[:]).then_inc(s_ewc, 1)

            link.leave(1, link.k)
            ew_chunk(0, 0)
            link.leave(1, 2)

            def gather_pass(k, r0, r1, ix, rank, carry, weight, extra=None, end=None):
                with rounds(dve, r0, r1) as i:
                    for u in range(U):
                        if u % HU == 0:
                            half = slice(u, u + HU)
                            dve.wait_ge(s_done, k * ET + i * U + u + HU)
                            if ix is not None:
                                V.tensor_copy(ixr[:, half], ix[:, bass.ds(i * U + u, HU)])
                            V.tensor_copy(crr[:, half], carry[:, bass.ds(i * U + u, HU)]).then_inc(s_idx, 1)
                        of = rank[:, bass.ds(i * U + u, 1)]
                        if weight is None:
                            ins = V.tensor_scalar(M[:, u, :], irow[:], of, None, ALU.is_equal)
                        else:
                            ins = V.tensor_scalar(M[:, u, :], irow[:], of, weight[:, bass.ds(i * U + u, 1)],
                                                  ALU.is_equal, ALU.mult)
                        ins.then_inc(s_m, 1)
                        if extra:
                            extra(i, u)
                    if end:
                        end(i)

            def one_hots(t, lo, hi, to, ql, qh):
                V.tensor_scalar(to[:, ql, :], irow_b[:], lo[:, bass.ds(t, 1)], None, ALU.is_equal)
                return V.tensor_scalar(hi_b[:, qh, :], irow_b[:, 0:NT], hi[:, bass.ds(t, 1)], None, ALU.is_equal)

            def count(i, u):
                t = i * U + u
                dve.wait_ge(s_cnt, t + 1)
                if u % 4 == 0:
                    for to, hi in ((hi_b, s_hi), (hi_d, d_hi)):
                        V.tensor_tensor(to[:, u % 8:u % 8 + 4, :],
                                        irow[:, 0:NT].rearrange("p (k c) -> p k c", k=1)
                                        .broadcast_to((P, 4, NT)),
                                        hi[:, bass.ds(t, 4)].rearrange("p (k c) -> p k c", c=1)
                                        .broadcast_to((P, 4, NT)), ALU.is_equal)
                V.tensor_scalar(lo_b[:, u % 4, :], irow_b[:], s_lo[:, bass.ds(t, 1)], None, ALU.is_equal)
                V.tensor_scalar(loT_b[:, u % 4, :], irow_b[:], d_lo[:, bass.ds(t, 1)], None, ALU.is_equal) \
                    .then_inc(s_oh, 1)

            def place(i, u):
                t = i * VU + u
                back = u if first_round(i) else VU
                if u < VU:
                    if back >= 4:
                        dve.wait_ge(s_pp, t - 3)
                    one_hots(t, s_lo, s_hi, lo_b, u % 4, u).then_inc(s_oh, 1)
                if back >= 2 and u < VU + 2:
                    v = (u - 2) % VU
                    dve.wait_ge(s_eq, 1 + t - 1)
                    V.tensor_tensor(eqm[:, v % 4, :], ps[:, 7, 0:P], before[:], ALU.mult).then_inc(s_eqm, 1)
                if back >= 4 and u < VU + 4:
                    v = (u - 4) % VU
                    dve.wait_ge(s_pp, t - 3)
                    dve.wait_ge(s_pos, 1 + t - 4)
                    if v == 0 and not (isinstance(i, int) and i == 0):
                        dve.wait_ge(s_posw, i)
                    V.tensor_tensor_reduce(junk[:], hi_b[:, v, :], ps[:, 5, 0:NT], 1.0, 0.0,
                                           ALU.mult, ALU.add, posr[:, v:v + 1]).then_inc(s_pos, 1)
                    if v == VU - 1:
                        dve.wait_ge(s_pos, 1 + t - 3)
                        V.tensor_copy(pos[:, bass.ds(t - 3 - VU, VU)], posr[:]).then_inc(s_posw, 1)

            def count_and_weigh(i):
                ew_chunk(i + 1, i)

            gather_pass(PASS_L0, 0, NR, None, rank_d, carry_d, w_f, count, count_and_weigh)
            link.leave(NR, 2)
            dve.wait_ge(s_ewc, EW_CHUNKS)
            V.memset(raw4[:, 3, NB - 1, :], 0.0).then_inc(s_sm, 1)

            def ends(side, n):
                ready(V.tensor_copy(n[:], ps[:, (7, 6)[side], 0:NT]))
                unit_done()
                link(V.tensor_copy(tot[:, side:side + 1], ps[0:NT, 4, 0:1]))
                ready(V.tensor_scalar(tot_b[:, side, :], ones[0:NT, :], tot[:, side:side + 1], None, ALU.mult))
                unit_done()
                e, lo_i, hi_i = small_i[:, 0, :], small_i[:, 1, :], small_i[:, 2, :]
                link(V.tensor_copy(base[:, side, :], ps[:, (5, 6)[side], 0:NT]))
                link(V.scalar_tensor_tensor(small[:, 0, :], base[:, side, :], -1.0, n[:], ALU.add, ALU.add))
                link(V.tensor_scalar(last_e[:, side, :], small[:, 0, :], 0.0, None, ALU.max))
                link(V.tensor_copy(e, last_e[:, side, :]))
                V.tensor_single_scalar(lo_i, e, P - 1, ALU.bitwise_and)
                link(V.tensor_single_scalar(hi_i, e, 7, ALU.logical_shift_right))
                V.tensor_copy(small[:, 1, :], lo_i)
                link(V.tensor_copy(small[:, 2, :], hi_i))
                V.scalar_tensor_tensor(end_ix[:, side, :], small[:, 1, :], float(ET), small[:, 2, :],
                                       ALU.mult, ALU.add).then_inc(s_eix, 1)
                link(V.tensor_scalar(last_e[:, side, :], small[:, 2, :], float(P), None, ALU.mult))

            def find_rows(side, n):
                dve.wait_ge(s_eg[side], 16 * NT)
                V.tensor_scalar(small[:, 0, :], n[:], 0.0, None, ALU.is_gt)
                link(V.scalar_tensor_tensor(small[:, 1, :], last_e[:, side, :], -float(ZROW), rank_end[:, side, :],
                                            ALU.add, ALU.add))
                link(V.tensor_tensor(small[:, 2, :], small[:, 1, :], small[:, 0, :], ALU.mult))
                V.tensor_scalar(fin[:, side, :], small[:, 2, :], float(ZROW), None, ALU.add).then_inc(s_tab, 1)

            dve.wait_ge(s_cnt, 4 + ET)
            dve.wait_ge(s_pc, 4 + ET)
            ends(0, n_d)
            link(V.tensor_scalar(eps1[:], eps_c[:], 1.0, None, ALU.add))
            dve.wait_ge(s_meta[3], 96)
            signal(s_rdy)
            unit_done()
            link(from_pair(w_f[:], 1))
            find_rows(0, n_d)
            link.leave(1, link.k)

            def flat(t):
                return t[:, :, :].rearrange("p j d -> p (j d)")

            def xg(i):
                return group(X, i).rearrange("p j d -> p (j d)")

            def n0_x(i, slot, nth):
                first.turn(i, 2)
                wait_group(dve, N0, slot, nth)
                ins = V.tensor_tensor(xg(i), xg(i), flat(AG[slot]), ALU.add)
                first(ins)
                V.sem_inc(s_a7, 1)
                first(V.scalar_tensor_tensor(xg(i), group(HN, i).rearrange("p j d -> p (j d)"), eps1[:], xg(i),
                                             ALU.mult, ALU.add))
                norm_step(N0, i)

            def rows_copy(ph):
                def step(i):
                    dve.wait_ge(s_a5, b("a5", ph) + i + 1)
                    dve.wait_ge(s_hst, 16 * (stores(ph) + i))
                    V.tensor_copy(flat(HS), bank(5)).then_inc(s_a6, 1)
                return step

            staged_by_two(dve, [(0, n0_x, True), (2, rows_copy(N0))])
            first.leave(NG, 2)
            norm.leave(NG, 2)

            ends(1, n_s)
            link(V.tensor_scalar(small[:, 3, :], n_s[:], 1.0, None, ALU.max))
            link(V.reciprocal(inv_s[:], small[:, 3, :]))
            link.leave(1, link.k)

            def relation(i):
                at = big[:, bass.ds(i * D, D)]
                link.turn(i, B)
                for m in range(B):
                    c = comp_b[:, bass.ds(i * B + m, 1)]
                    if m == 0:
                        link(V.tensor_scalar(at, basis[:, m, :], c, None, ALU.mult))
                    else:
                        link(V.scalar_tensor_tensor(at, basis[:, m, :], c, at, ALU.mult, ALU.add))

            for l in range(LAYERS):
                k = PASS_L1 + l
                args = (None, rank_d, carry_d, w_f)
                if k in PLACE:
                    def pass_of(k, r0, r1, extra):
                        gather_pass(k, r0, r1, *args, extra)
                    pass_with_places(pass_of, k, place)
                    drain(k, place)
                else:
                    gather_pass(k, 0, R, *args, end=relation)
                    link.leave(R, B)
                    gather_pass(k, R, NR, *args)
                ph = G0 + l

                def gru(i):
                    first.turn(i, 3)
                    dve.wait_ge(s_a3, b("a3", ph) + 3 * i + 2)
                    dve.wait_ge(s_a4, b("a4", ph) + 3 * i + 1)
                    first(V.scalar_tensor_tensor(tS[:], bank(3), b_hh[:, 2:3], rS[:], ALU.add, ALU.mult))
                    V.tensor_tensor(tS[:], tS[:], bank(2), ALU.add).then_inc(s_a8, 1)
                    dve.wait_ge(s_a4, b("a4", ph) + 3 * i + 3)
                    dve.wait_ge(s_a5, b("a5", ph) + i)
                    if l < LAYERS - 1:
                        dve.wait_ge(s_a10, b("a10", ph) + i)
                    first(V.tensor_tensor(dS, feat(i), nS[:], ALU.subtract))
                    first(V.tensor_tensor(dS, dS, zS[:], ALU.mult))
                    V.tensor_tensor(dS, dS, nS[:], ALU.add).then_inc(s_a8, 1)

                def gru_x(i):
                    dve.wait_ge(s_a5, b("a5", ph) + i + 1)
                    x_add(i)
                    norm_step(G2, i)

                def x_add(i):
                    last.turn(i, 1)
                    last(V.tensor_tensor(xg(i), xg(i), bank(5), ALU.add))
                    V.sem_inc(s_a7, 1)

                last = Chain(s_v2)
                if l < LAYERS - 1:
                    staged(dve, [(0, gru), (1, rows_copy(ph))])
                else:
                    staged(dve, [(0, gru), (1, gru_x)])
                    norm.leave(NG, 2)
                first.leave(NG, 3)

            dve.wait_ge(s_eg[2], 32)
            signal(s_rdy)
            unit_done()
            V.tensor_copy(erT[0:P, 0:2, :], ps[:, 4, 0:2 * R].rearrange("p (c r) -> p c r", r=R))
            ready(V.tensor_copy(erT[0:2 * DA, 2, :], ps[0:2 * DA, 4, 2 * R:3 * R]))
            unit_done()
            link(V.tensor_tensor(ahid[:, 0, :], ps[0:R, 5, 0:D], ab1[:], ALU.add))
            link(V.tensor_scalar(ahid[:, 0, :], ahid[:, 0, :], 0.0, None, ALU.max))
            V.tensor_tensor_reduce(ahid[:, 1, :], ahid[:, 0, :], aw2[:], 1.0, 0.0, ALU.mult, ALU.add,
                                   alog[:, 0:1]).then_inc(s_att, 1)
            dve.wait_ge(s_att, 2)
            ready(V.tensor_scalar(adiag[:], ident[0:R, 0:R], alog[:, 1:2], None, ALU.mult))
            unit_done()
            link(V.tensor_copy(alpha[:], ps[:, 4, 64:64 + R]))
            for r in range(R):
                ins = V.tensor_scalar(big[:, r * D:(r + 1) * D], big[:, r * D:(r + 1) * D], alpha[:, r:r + 1],
                                      None, ALU.mult)
            ready(ins)
            link.leave(1, link.k)

            with dve.Fori(0, NT // 2) as i:
                for q in range(2):
                    dve.wait_ge(s_tm, i * 2 + q + 1)
                    dve.wait_ge(s_ts[q], 16 * (1 + i))
                    V.tensor_copy(t_buf[q][:, 2 * BANK:4 * BANK], ps[:, 4 * q + 2:4 * q + 4, :]
                                  .rearrange("p b c -> p (b c)")).then_inc(s_te[1], 1)
            for q in range(2):
                dve.wait_ge(s_ts[q], 16 * (1 + NT // 2))
            gather_pass(PASS_L2, 0, PREP_AT, ix_t, rank_d, carry_d, None)
            dve.wait_ge(s_meta[0], 64)
            for k in range(2):
                ready(V.tensor_copy(flt[k], raw_pair[:, :, :, k]))
            unit_done()
            link(from_pair(src_f, 2))
            unit_done()
            link(from_pair(dst_f, 3))
            ready(V.tensor_copy(ix_q[:], dst_f))
            segments(src_f, carry_s[:], rank_s[:], 2, 3, s_sm)
            link.leave(1, link.k)
            gather_pass(PASS_L2, PREP_AT, NR, ix_t, rank_d, carry_d, None)
            find_rows(1, n_s)
            link.leave(1, link.k)

            def n2_x(i, slot, nth):
                first.turn(i, 2)
                wait_group(dve, N2, slot, nth)
                dve.wait_ge(s_a3, b("a3", N2) + i + 1)
                for j in range(GN):
                    ins = V.scalar_tensor_tensor(tS[:, j * D:(j + 1) * D], ps[:, 0, j * D:(j + 1) * D],
                                                 n_d[:, bass.ds(i * GN + j, 1)], AG[slot][:, j, :],
                                                 ALU.mult, ALU.add)
                first(ins)
                V.sem_inc(s_a7, 1)
                first(V.scalar_tensor_tensor(xg(i), tS[:], 0.0, xg(i), ALU.max, ALU.add))
                norm_step(N2, i)

            staged_by_two(dve, [(0, n2_x, True)])
            first.leave(NG, 2)
            norm.leave(NG, 2)
            gather_pass(PASS_L3, 0, NR, ix_q, rank_s, carry_s, None)

            def n3_y(i, slot, nth):
                wait_group(dve, N3, slot, nth)
                dve.wait_ge(s_a1, b("a1", N3) + i)
                for j in range(GN):
                    ins = V.scalar_tensor_tensor(HG[:, j, :], AG[slot][:, j, :], inv_s[:, bass.ds(i * GN + j, 1)],
                                                 HN[:, bass.ds(i * GN + j, 1), :].rearrange("p t d -> p (t d)"),
                                                 ALU.mult, ALU.add)
                ins.then_inc(s_a8, 1)
                dve.wait_ge(s_a8, b("a8", N3) + i + 1)
                V.sem_inc(s_a7, 1)

            def n3_out(i):
                first.turn(i, 1)
                dve.wait_ge(s_a3, b("a3", N3) + i + 1)
                dve.wait_ge(s_hst, 16 * (stores(N3) + i))
                for j in range(GN):
                    ins = V.tensor_tensor(HS[:, j, :], ps[:, 0, j * D:(j + 1) * D], b3[:], ALU.add)
                first(ins)
                V.tensor_tensor(flat(HS), flat(HS), xg(i), ALU.add).then_inc(s_a6, 1)

            staged_by_two(dve, [(0, n3_y, True), (1, n3_out)])

        @block.scalar
        def _(act):
            A = nc.scalar

            def hold(s, value):
                act.wait_ge(s, value)
                act.sem_inc(s_hold[2], 1)

            act.sem_inc(s_pc, 4)
            for s in (s_hg, s_a2, s_a4, s_a10, s_lc, s_te[0]):
                act.sem_inc(s, 1)

            def normalise(ph, dst, free=None):
                def step(i):
                    hold(s_ln, b("ln", ph) + i + 1)
                    if free:
                        free(i)
                    for j in range(GN):
                        ins = A.activation(dst(i, j), X[:, bass.ds(i * GN + j, 1), :].rearrange("p t d -> p (t d)"),
                                           ACT.Relu, bias=nbias[:, bass.ds(i * GN + j, 1)],
                                           scale=rstd[:, bass.ds(i * GN + j, 1)])
                    ins.then_inc(s_hg, 1)
                return step

            def into_hn(i, j):
                return HN[:, bass.ds(i * GN + j, 1), :].rearrange("p t d -> p (t d)")

            def into_hg(i, j):
                return HG[:, j, :]

            act.wait_ge(s_sm, 1)
            with act.Fori(0, NG) as i:
                normalise(LN0, into_hn)(i)

            def gather_pass(k, r0, r1, extra=None):
                with rounds(act, r0, r1) as i:
                    for u in range(U):
                        if u % HU == 0:
                            act.wait_ge(s_ps[u // HU], 16 * (1 + k * NR + i))
                        act.wait_ge(s_done, U + k * ET + i * U + u + 1)
                        A.copy(PR[:, u, :], ps[:, u % 4, 0:D]).then_inc(s_pc, 1)
                        if extra:
                            extra(i, u)

            def place(i, u):
                t = i * VU + u
                act.wait_ge(s_loT, t + 1)
                if u >= 4 or not first_round(i):
                    act.wait_ge(s_pp, t - 3)
                A.copy(loT[:, u % 4, :], ps[:, 4, 0:P // 2].bitcast(BF16))
                act.wait_ge(s_eq, 1 + t)
                A.copy(run_s[:, u % 4, :], ps[:, 6, 0:NT]).then_inc(s_lc, 1)

            def copy_in(ph):
                def step(i):
                    act.wait_ge(s_a1, b("a1", ph) + i + 1)
                    if ph in (N0, N3):
                        if not (isinstance(i, int) and i == 0):
                            act.wait_ge(s_a3, b("a3", ph) + i)
                    elif not (isinstance(i, int) and i == 0):
                        act.wait_ge(s_a3, b("a3", ph) + 3 * i)
                    A.copy(aT[:], bank(4)).then_inc(s_a2, 1)
                return step

            gather_pass(PASS_L0, 0, NR)

            def hg_free(i):
                act.wait_ge(s_a1, b("a1", N0) + i)

            def n0_relu(i):
                act.wait_ge(s_a5, b("a5", N0) + i)
                hold(s_a3, b("a3", N0) + i + 1)
                A.activation(dS, bank(0), ACT.Relu, bias=b_node[:]).then_inc(s_a4, 1)
                A.activation(feat(i), bank(0), ACT.Relu, bias=b_node[:]).then_inc(s_a10, 1)

            staged(act, [(0, normalise(N0, into_hg, hg_free)), (0, copy_in(N0)), (1, n0_relu)])
            for l in range(LAYERS):
                k = PASS_L1 + l
                if k in PLACE:
                    pass_with_places(gather_pass, k, place)
                else:
                    gather_pass(k, 0, NR)
                ph = G0 + l

                def gates(i):
                    act.wait_ge(s_a3, b("a3", ph) + 3 * i + 1)
                    if not (isinstance(i, int) and i == 0):
                        act.wait_ge(s_a8, b("a8", ph) + 2 * i)
                    A.activation(rS[:], bank(0), ACT.Sigmoid, bias=b_rz[:, 0:1]).then_inc(s_a4, 1)
                    act.wait_ge(s_a3, b("a3", ph) + 3 * i + 3)
                    A.activation(zS[:], bank(1), ACT.Sigmoid, bias=b_rz[:, 1:2]).then_inc(s_a4, 1)
                    act.wait_ge(s_a8, b("a8", ph) + 2 * i + 1)
                    A.activation(nS[:], tS[:], ACT.Tanh, bias=b_ih[:, 2:3]).then_inc(s_a4, 1)

                def keep(i):
                    hold(s_a8, b("a8", ph) + 2 * i + 2)
                    A.copy(feat(i), dS).then_inc(s_a10, 1)

                stages = [(0, copy_in(ph))] + ([(1, keep)] if l < LAYERS - 1 else []) + [(0, gates)]
                if l == LAYERS - 1:
                    def hg_used(i):
                        if not (isinstance(i, int) and i == 0):
                            act.wait_ge(s_a9, b("a9", G2) + i)
                        act.wait_ge(s_hst, 16 * (stores(G2) + i))

                    def next_copy(i):
                        hold(s_a9, b("a9", G2) + i + 1)
                        A.copy(feat(i), bank(6)).then_inc(s_a10, 1)

                    stages += [(1, normalise(G2, into_hg, hg_used)), (2, next_copy)]
                staged(act, stages)
            act.wait_ge(s_att, 1)
            A.activation(alog[:, 1:2], alog[:, 0:1], ACT.Sigmoid, bias=ab2[:]).then_inc(s_att, 1)
            def table_h(i, q):
                A.copy(dS[:, q * P:(q + 1) * P], HT[:, bass.ds((2 * i + q) * P, P)]).then_inc(s_th, 1)

            for q in range(2):
                table_h(0, q)
            def table_out(i, last=False):
                for q in range(2):
                    hold(s_tm, i * 2 + q + 1)
                    if not last:
                        table_h(i + 1, q)
                    act.wait_ge(s_ts[q], 16 * (1 + i))
                    A.copy(t_buf[q][:, 0:2 * BANK], ps[:, 4 * q:4 * q + 2, :].rearrange("p b c -> p (b c)")) \
                        .then_inc(s_te[0], 1)

            with act.Fori(0, NT // 2 - 1) as i:
                table_out(i)
            table_out(NT // 2 - 1, last=True)
            gather_pass(PASS_L2, 0, NR)

            def update_in(i):
                hold(s_a3, b("a3", N2) + i)
                A.copy(aT[:], feat(i)).then_inc(s_a2, 1)

            staged(act, [(0, update_in), (1, normalise(N2, into_hn))])
            gather_pass(PASS_L3, 0, NR)
            staged(act, [(0, copy_in(N3))])


_INS = ["x", "src", "dst", "edge_attr_32", "edge_attr_32_n2", "edge_attr_64", "edge_attr_64_n2",
        "edge_type_16", "edge_weight", "L0_gnn_eps", "L1_gnn_W_node", "L1_gnn_b_node",
        "L1_gnn_conv_weight", "L1_gnn_w_ih", "L1_gnn_w_hh", "L1_gnn_b_ih", "L1_gnn_b_hh",
        "L2_gnn_weight", "L2_gnn_comp", "L2_gnn_attn_w1", "L2_gnn_attn_b1", "L2_gnn_attn_w2",
        "L2_gnn_attn_b2", "L2_gnn_update", "L3_gnn_W", "L3_gnn_b"]


def kernel(**inputs):
    import numpy as _np
    import concourse.bacc as _bacc
    from concourse import mybir as _mybir
    from concourse.bass_utils import run_bass_kernel_spmd as _run

    nc = _bacc.Bacc("TRN2", target_bir_lowering=False, num_devices=1)
    arrays, aps = {}, {}
    for name in _INS:
        v = _np.ascontiguousarray(inputs[name])
        arrays[f"in_{name}"] = v
        aps[name] = nc.dram_tensor(f"in_{name}", v.shape, _mybir.dt.from_np(v.dtype), kind="ExternalInput").ap()
    out = nc.dram_tensor("out_x", (N, D), F32, kind="ExternalOutput").ap()
    gnn_kernel(nc, aps, out)
    r = _run(nc, [arrays], core_ids=[0])
    return r.results[0]["out_x"]
```
